# Optimizing a Trainium2 kernel written in Bass

```python
import numpy as np
import jax
import jax.numpy as jnp

def _softmax(x, axis=-1):
    return jax.nn.softmax(x, axis=axis)

def _gelu(x):
    return jax.nn.gelu(x, approximate=True)

def _silu(x):
    return jax.nn.silu(x)

def _sigmoid(x):
    return jax.nn.sigmoid(x)

def _layernorm(x, axis=-1, eps=1e-05):
    m = jnp.mean(x, axis=axis, keepdims=True)
    v = jnp.var(x, axis=axis, keepdims=True)
    return (x - m) / jnp.sqrt(v + eps)

def _scatter_add(tgt, idx, src, axis=0):
    return tgt.at[idx].add(src)

def _segment_sum(src, seg, n):
    return jax.ops.segment_sum(src, seg, n)
kernel_name = 'mk_conv_seq_d2_conv_nhwc512_r4_cb8d41'

def setup_inputs(seed: int=0):
    np.random.seed(seed)
    _w = jnp.asarray

    def _rec_inputs():
        import jax
        import jax.numpy as jnp
        _gk = jax.random.key(seed)
        x = 7.22e-05 + 1 * jax.random.normal(jax.random.fold_in(_gk, 1), (4, 16, 16, 128), jnp.float32)
        return x
    x = _rec_inputs()

    def _L0_conv_setup():
        import jax, jax.numpy as jnp
        import numpy as np
        B, H, W, C = (4, 16, 16, 128)
        R, NH, KS = (2, 8, 7)
        S = 1.0

        def layernorm(t, g, b):
            m = t.mean(-1, keepdims=True)
            v = ((t - m) ** 2).mean(-1, keepdims=True)
            return (t - m) / jnp.sqrt(v + 1e-05) * g + b

        def grid_sample_bilinear_zeros(img, grid):
            b, c, h, w = img.shape
            gh, gw = (grid.shape[1], grid.shape[2])
            x = (grid[..., 0] + 1.0) * 0.5 * (w - 1)
            y = (grid[..., 1] + 1.0) * 0.5 * (h - 1)
            x0 = jnp.floor(x)
            y0 = jnp.floor(y)
            wx1 = x - x0
            wy1 = y - y0
            x0i = x0.astype(jnp.int32)
            y0i = y0.astype(jnp.int32)
            flat = img.reshape(b, c, h * w)

            def corner(xi, yi, wt):
                valid = ((xi >= 0) & (xi < w) & (yi >= 0) & (yi < h)).astype(img.dtype)
                idx = jnp.clip(yi, 0, h - 1) * w + jnp.clip(xi, 0, w - 1)
                vals = jnp.take_along_axis(flat, idx.reshape(b, 1, gh * gw), axis=2)
                return vals * (valid * wt).reshape(b, 1, gh * gw)
            out = corner(x0i, y0i, (1 - wx1) * (1 - wy1)) + corner(x0i + 1, y0i, wx1 * (1 - wy1)) + corner(x0i, y0i + 1, (1 - wx1) * wy1) + corner(x0i + 1, y0i + 1, wx1 * wy1)
            return out.reshape(b, c, gh, gw)
        key = jax.random.key(seed)
        ks = jax.random.split(key, 12)
        sd = 0.02
        f32 = jnp.float32
        return {'x': jax.random.normal(ks[0], (B, H, W, C), f32), 'ln_g': jnp.ones((C,), f32), 'ln_b': jnp.zeros((C,), f32), 'wq': jax.random.normal(ks[1], (C, C), f32) * sd, 'bq': jnp.zeros((C,), f32), 'wv': jax.random.normal(ks[2], (C, C), f32) * sd, 'bv': jnp.zeros((C,), f32), 'dw_w': jax.random.normal(ks[3], (C, 1, KS, KS), f32) * sd, 'dw_b': jnp.zeros((C,), f32), 'pw_w': jax.random.normal(ks[4], (2, C, 1, 1), f32) * sd, 'mq_w': jax.random.normal(ks[5], (C, C), f32) * sd, 'mq_b': jnp.zeros((C,), f32), 'mk_w': jax.random.normal(ks[6], (C, C), f32) * sd, 'mk_b': jnp.zeros((C,), f32), 'mv_w': jax.random.normal(ks[7], (C, C), f32) * sd, 'mv_b': jnp.zeros((C,), f32), 'mo_w': jax.random.normal(ks[8], (C, C), f32) * sd, 'mo_b': jnp.zeros((C,), f32), 'mlp_w': jax.random.normal(ks[9], (C, C), f32) * sd, 'mlp_b': jnp.zeros((C,), f32)}
    _L0_conv_all = _L0_conv_setup()
    _L0_conv_in = {k: v for k, v in _L0_conv_all.items() if k in ('ln_g', 'ln_b', 'wq', 'bq', 'wv', 'bv', 'dw_w', 'dw_b', 'pw_w', 'mq_w', 'mq_b', 'mk_w', 'mk_b', 'mv_w', 'mv_b', 'mo_w', 'mo_b', 'mlp_w', 'mlp_b')}
    del _L0_conv_all

    def _L1_conv_setup():
        import jax, jax.numpy as jnp
        import numpy as np
        SPARSITY = 0.01

        def _cas(n):
            t = jnp.arange(n, dtype=jnp.float32)
            a = 2.0 * jnp.pi * jnp.outer(t, t) / n
            return jnp.cos(a) + jnp.sin(a)

        def _dht2d(x):
            B, H, W, C = x.shape
            y = jnp.einsum('bhwc,cd->bhwd', x, _cas(C))
            return jnp.einsum('vw,bhwd->bhvd', _cas(W), y)
        key = jax.random.key(seed)
        k0, k1, k2, k3, k4 = jax.random.split(key, 5)
        B, H, W, C = (1, 45, 90, 128)
        nb, bs, f = (8, 16, 1)
        scale = 0.02
        x = jax.random.normal(k0, (B, H, W, C), jnp.float32)
        w1 = scale * jax.random.normal(k1, (2, nb, bs, bs * f), jnp.float32)
        b1 = scale * jax.random.normal(k2, (2, nb, bs * f), jnp.float32)
        w2 = scale * jax.random.normal(k3, (2, nb, bs * f, bs), jnp.float32)
        b2 = scale * jax.random.normal(k4, (2, nb, bs), jnp.float32)
        return {'x': x, 'w1': w1, 'b1': b1, 'w2': w2, 'b2': b2}
    _L1_conv_all = _L1_conv_setup()
    _L1_conv_in = {k: v for k, v in _L1_conv_all.items() if k in ('w1', 'b1', 'w2', 'b2')}
    del _L1_conv_all
    return {'x': x, 'L0_conv_ln_g': _L0_conv_in['ln_g'], 'L0_conv_ln_b': _L0_conv_in['ln_b'], 'L0_conv_wq': _L0_conv_in['wq'], 'L0_conv_bq': _L0_conv_in['bq'], 'L0_conv_wv': _L0_conv_in['wv'], 'L0_conv_bv': _L0_conv_in['bv'], 'L0_conv_dw_w': _L0_conv_in['dw_w'], 'L0_conv_dw_b': _L0_conv_in['dw_b'], 'L0_conv_pw_w': _L0_conv_in['pw_w'], 'L0_conv_mq_w': _L0_conv_in['mq_w'], 'L0_conv_mq_b': _L0_conv_in['mq_b'], 'L0_conv_mk_w': _L0_conv_in['mk_w'], 'L0_conv_mk_b': _L0_conv_in['mk_b'], 'L0_conv_mv_w': _L0_conv_in['mv_w'], 'L0_conv_mv_b': _L0_conv_in['mv_b'], 'L0_conv_mo_w': _L0_conv_in['mo_w'], 'L0_conv_mo_b': _L0_conv_in['mo_b'], 'L0_conv_mlp_w': _L0_conv_in['mlp_w'], 'L0_conv_mlp_b': _L0_conv_in['mlp_b'], 'L1_conv_w1': _L1_conv_in['w1'], 'L1_conv_b1': _L1_conv_in['b1'], 'L1_conv_w2': _L1_conv_in['w2'], 'L1_conv_b2': _L1_conv_in['b2']}

def reference(x, L0_conv_ln_g, L0_conv_ln_b, L0_conv_wq, L0_conv_bq, L0_conv_wv, L0_conv_bv, L0_conv_dw_w, L0_conv_dw_b, L0_conv_pw_w, L0_conv_mq_w, L0_conv_mq_b, L0_conv_mk_w, L0_conv_mk_b, L0_conv_mv_w, L0_conv_mv_b, L0_conv_mo_w, L0_conv_mo_b, L0_conv_mlp_w, L0_conv_mlp_b, L1_conv_w1, L1_conv_b1, L1_conv_w2, L1_conv_b2):
    import jax
    import jax.numpy as jnp

    def _L0_conv_ref(x, ln_g, ln_b, wq, bq, wv, bv, dw_w, dw_b, pw_w, mq_w, mq_b, mk_w, mk_b, mv_w, mv_b, mo_w, mo_b, mlp_w, mlp_b):
        import jax, jax.numpy as jnp
        import numpy as np
        B, H, W, C = (4, 16, 16, 128)
        R, NH, KS = (2, 8, 7)
        S = 1.0

        def layernorm(t, g, b):
            m = t.mean(-1, keepdims=True)
            v = ((t - m) ** 2).mean(-1, keepdims=True)
            return (t - m) / jnp.sqrt(v + 1e-05) * g + b

        def grid_sample_bilinear_zeros(img, grid):
            b, c, h, w = img.shape
            gh, gw = (grid.shape[1], grid.shape[2])
            x = (grid[..., 0] + 1.0) * 0.5 * (w - 1)
            y = (grid[..., 1] + 1.0) * 0.5 * (h - 1)
            x0 = jnp.floor(x)
            y0 = jnp.floor(y)
            wx1 = x - x0
            wy1 = y - y0
            x0i = x0.astype(jnp.int32)
            y0i = y0.astype(jnp.int32)
            flat = img.reshape(b, c, h * w)

            def corner(xi, yi, wt):
                valid = ((xi >= 0) & (xi < w) & (yi >= 0) & (yi < h)).astype(img.dtype)
                idx = jnp.clip(yi, 0, h - 1) * w + jnp.clip(xi, 0, w - 1)
                vals = jnp.take_along_axis(flat, idx.reshape(b, 1, gh * gw), axis=2)
                return vals * (valid * wt).reshape(b, 1, gh * gw)
            out = corner(x0i, y0i, (1 - wx1) * (1 - wy1)) + corner(x0i + 1, y0i, wx1 * (1 - wy1)) + corner(x0i, y0i + 1, (1 - wx1) * wy1) + corner(x0i + 1, y0i + 1, wx1 * wy1)
            return out.reshape(b, c, gh, gw)
        b, h, w, c = x.shape
        x_ln = layernorm(x, ln_g, ln_b).transpose(0, 3, 1, 2)
        x_flat = x_ln.reshape(b, h * w, c)
        q = x_flat @ wq + bq
        q_img = q.reshape(b, c, h, w)
        o = jax.lax.conv_general_dilated(q_img, dw_w, (R, R), [(KS // 2, KS // 2)] * 2, dimension_numbers=('NCHW', 'OIHW', 'NCHW'), feature_group_count=c)
        o = jax.nn.gelu(o + dw_b[None, :, None, None], approximate=False)
        offsets = jax.lax.conv_general_dilated(o, pw_w, (1, 1), [(0, 0), (0, 0)], dimension_numbers=('NCHW', 'OIHW', 'NCHW'))
        hg, wg = (offsets.shape[2], offsets.shape[3])
        ref_x = (jnp.arange(wg, dtype=x.dtype) + 0.5) * (2.0 / wg) - 1.0
        ref_y = (jnp.arange(hg, dtype=x.dtype) + 0.5) * (2.0 / hg) - 1.0
        gx, gy = jnp.meshgrid(ref_x, ref_y, indexing='ij')
        refs = jnp.stack([gx, gy], axis=0)
        deformed = refs[None] + S * jnp.tanh(offsets)
        deformed = (deformed + 1.0) * (h / R) / 2.0
        grid = deformed[:, ::-1].transpose(0, 2, 3, 1)
        interp = grid_sample_bilinear_zeros(x.transpose(0, 3, 1, 2), grid)
        interp_flat = interp.reshape(b, hg * wg, c)
        v = interp_flat @ wv + bv
        k = interp_flat @ wv + bv
        hd = c // NH

        def heads(t):
            return t.reshape(b, -1, NH, hd).transpose(0, 2, 1, 3)
        qh = heads(q @ mq_w + mq_b)
        kh = heads(k @ mk_w + mk_b)
        vh = heads(v @ mv_w + mv_b)
        attn = jax.nn.softmax(jnp.einsum('bnqd,bnkd->bnqk', qh, kh), axis=-1)
        att = jnp.einsum('bnqk,bnkd->bnqd', attn, vh).transpose(0, 2, 1, 3).reshape(b, h * w, c)
        msa = att @ mo_w + mo_b
        z = msa + x.reshape(b, h * w, c)
        z_ln = layernorm(z, ln_g, ln_b)
        out = jax.nn.gelu(z_ln @ mlp_w + mlp_b, approximate=False) + z
        return out.reshape(b, w, h, c)

    def _L1_conv_ref(x, w1, b1, w2, b2):
        import jax, jax.numpy as jnp
        import numpy as np
        SPARSITY = 0.01

        def _cas(n):
            t = jnp.arange(n, dtype=jnp.float32)
            a = 2.0 * jnp.pi * jnp.outer(t, t) / n
            return jnp.cos(a) + jnp.sin(a)

        def _dht2d(x):
            B, H, W, C = x.shape
            y = jnp.einsum('bhwc,cd->bhwd', x, _cas(C))
            return jnp.einsum('vw,bhwd->bhvd', _cas(W), y)
        bias = x
        B, H, W, C = x.shape
        nb, bs = (w1.shape[1], w1.shape[2])
        xh = _dht2d(x).reshape(B, H, W, nb, bs)
        xn = jnp.roll(jnp.flip(xh, axis=(1, 2)), shift=(1, 1), axis=(1, 2))
        w1a, w1b = (w1[0] + w1[1], w1[0] - w1[1])
        o1k = jax.nn.relu(0.5 * (jnp.einsum('bhwki,kio->bhwko', xh, w1a) + jnp.einsum('bhwki,kio->bhwko', xn, w1b)) + b1[0])
        o1n = jax.nn.relu(0.5 * (jnp.einsum('bhwki,kio->bhwko', xn, w1a) + jnp.einsum('bhwki,kio->bhwko', xh, w1b)) + b1[1])
        w2a, w2b = (w2[0] + w2[1], w2[0] - w2[1])
        o2k = 0.5 * (jnp.einsum('bhwki,kio->bhwko', o1k, w2a) + jnp.einsum('bhwki,kio->bhwko', o1n, w2b)) + b2[0]
        o2n = 0.5 * (jnp.einsum('bhwki,kio->bhwko', o1n, w2a) + jnp.einsum('bhwki,kio->bhwko', o2k, w2b)) + b2[1]
        y = (o2k + o2n).reshape(B, H, W, C)
        y = jnp.sign(y) * jax.nn.relu(jnp.abs(y) - SPARSITY)
        y = _dht2d(y) / (W * C)
        return y + bias

    def _gn(v, G=32, eps=1e-05):
        B_, H_, W_, C_ = v.shape
        g = v.reshape(B_, H_, W_, G, C_ // G)
        m = jnp.mean(g, axis=(1, 2, 4), keepdims=True)
        s = jnp.var(g, axis=(1, 2, 4), keepdims=True)
        return ((g - m) / jnp.sqrt(s + eps)).reshape(v.shape)

    def _ln_c(v, eps=1e-06):
        m = jnp.mean(v, axis=-1, keepdims=True)
        s = jnp.var(v, axis=-1, keepdims=True)
        return (v - m) / jnp.sqrt(s + eps)

    def _ln_t(v, eps=1e-05):
        m = jnp.mean(v, axis=-1, keepdims=True)
        s = jnp.var(v, axis=-1, keepdims=True)
        return (v - m) / jnp.sqrt(s + eps)

    def _to_tokens(v):
        B_, H_, W_, C_ = v.shape
        return v.reshape(B_, H_ * W_, C_)

    def _from_tokens(t, like):
        return t.reshape(like.shape)
    x = _L0_conv_ref(x, L0_conv_ln_g, L0_conv_ln_b, L0_conv_wq, L0_conv_bq, L0_conv_wv, L0_conv_bv, L0_conv_dw_w, L0_conv_dw_b, L0_conv_pw_w, L0_conv_mq_w, L0_conv_mq_b, L0_conv_mk_w, L0_conv_mk_b, L0_conv_mv_w, L0_conv_mv_b, L0_conv_mo_w, L0_conv_mo_b, L0_conv_mlp_w, L0_conv_mlp_b)
    x = _L1_conv_ref(x, L1_conv_w1, L1_conv_b1, L1_conv_w2, L1_conv_b2)
    return x

_drawn_inputs = setup_inputs


def setup_inputs(seed=0):
    import zlib

    import numpy as np

    out = dict(_drawn_inputs(seed))
    spreads = {'L0_conv_ln_g': (1.0, 0.576),
     'L0_conv_ln_b': (0.0, 0.727),
     'L0_conv_bq': (0.0, 0.8),
     'L0_conv_bv': (0.0, 0.8),
     'L0_conv_dw_b': (0.0, 0.8),
     'L0_conv_mq_b': (0.0, 0.8),
     'L0_conv_mk_b': (0.0, 2.0),
     'L0_conv_mv_b': (0.0, 0.363),
     'L0_conv_mo_b': (0.0, 0.1),
     'L0_conv_mlp_b': (0.0, 0.1)}
    factors = {'L0_conv_wq': 8.0,
     'L0_conv_wv': 8.0,
     'L0_conv_dw_w': 8.0,
     'L0_conv_pw_w': 8.0,
     'L0_conv_mq_w': 8.0,
     'L0_conv_mk_w': 8.0,
     'L0_conv_mv_w': 8.0,
     'L1_conv_w1': 8.0,
     'L1_conv_b1': 200.0,
     'L1_conv_w2': 8.0,
     'L1_conv_b2': 64.0}
    for name, (base, spread) in spreads.items():
        noise = np.random.default_rng([zlib.crc32(name.encode()), seed]).standard_normal(out[name].shape)
        drawn = base * np.exp(spread * noise) if base else spread * noise
        out[name] = jnp.asarray(drawn.astype(out[name].dtype))
    for name, factor in factors.items():
        out[name] = (out[name] * factor).astype(out[name].dtype)
    return out
```

```python
from contextlib import ExitStack

import numpy as np

import concourse.bass as bass
from concourse import mybir

ALU = mybir.AluOpType
ACT = mybir.ActivationFunctionType
F32 = mybir.dt.float32
F32R = mybir.dt.float32r
AX_X = mybir.AxisListType.X

B, H, W, C = 4, 16, 16, 128
P = 128
HEADS, HD = 8, 16
KS, PAD, R = 7, 3, 2
HG = H // R
KEYS = HG * HG
TILES = B * 2
EPS = 1e-5
SPARSITY = 0.01
COORD = 4.0 * 0.5 * (W - 1)

CONST_W = {"ident": P, "wsd": 2 * P, "winv": 2 * P, "cas": P, "center": P, "dist": 3 * KEYS,
           "vmask": P, "rowsum": 32, "kmask": 4, "block": 8, "half": 8, "pick": 4 * P}
CONST = {}
_at = 0
for _name, _w in CONST_W.items():
    CONST[_name] = (_at, _at + _w)
    _at += _w
CONST_N = _at

VECTORS = ["ln_g", "ln_b", "dw_b", "bq", "bv", "mq_b", "mk_b", "mv_b", "b2n", "mo_b", "b1k", "b1n",
           "b2k", "pw0", "pw1"]
VEC = {n: i for i, n in enumerate(VECTORS)}
NTAP = KS * KS
EARLY_N = P + NTAP + len(VECTORS)
WEIGHTS = ["wqT", "mq", "wvT", "mk", "mv", "moT", "mlp"]
LATE = {n: (i * P, (i + 1) * P) for i, n in enumerate(WEIGHTS)}
_at = len(WEIGHTS) * P
for _name in ("w1", "w2", "w2T"):
    LATE[_name] = (_at, _at + 32)
    _at += 32
LATE["mo"] = (_at, _at + P)
LATE_N = _at + P
ROWS = ["ln_g", "ln_b", "bq_img", "mo_b", "mlp_b"]

def tile_tokens(par):
    return [(2 * h2 + par, 2 * w2 + half) for half in range(2) for h2 in range(8) for w2 in range(8)]


def frequency_pairs(par):
    first, fixed, second, seen = [], [], [], set()
    for h in range(par, H, 2):
        for v in range(W):
            a, b = (h, v), ((-h) % H, (-v) % W)
            if a in seen:
                continue
            seen |= {a, b}
            if a == b:
                fixed.append(a)
            else:
                first.append(a)
                second.append(b)
    return first, fixed, second


PAIRS = [len(frequency_pairs(par)[0]) for par in range(2)]
FIXED = [len(frequency_pairs(par)[1]) for par in range(2)]


def constants():
    c = {}
    eye = np.eye(P)
    c["ident"] = eye

    def cas(n):
        t = np.arange(n)
        a = 2.0 * np.pi * (np.outer(t, t) % n) / n
        return np.cos(a) + np.sin(a)

    cw = cas(W)
    wsd, winv = np.zeros((P, 2, P)), np.zeros((P, 2, P))
    for par in range(2):
        first, fixed, second = frequency_pairs(par)
        for row, (h, w) in enumerate(tile_tokens(par)):
            for n, (fh, fv) in enumerate(first + fixed):
                gh, gv = (-fh) % H, (-fv) % W
                s = cw[fv, w] * (fh == h) + cw[gv, w] * (gh == h)
                d = cw[fv, w] * (fh == h) - cw[gv, w] * (gh == h)
                wsd[row, par, n] = 0.5 * s
                if n < len(first):
                    wsd[row, par, len(first) + len(fixed) + n] = 0.5 * d
            for n, (fh, fv) in enumerate(first + fixed + second):
                winv[n, par, row] = cw[fv, w] * (fh == h) / (W * C)
    c["wsd"], c["winv"], c["cas"] = wsd, winv, cas(C)
    c["center"] = eye - 1.0 / C
    p = np.arange(P)[:, None]
    i, j = np.arange(KEYS)[None] // HG, np.arange(KEYS)[None] % HG
    dist = np.zeros((P, 3, KEYS))
    dist[:, 0] = (j + 1.5) * 0.5 * (W - 1) - p % W
    dist[:, 1] = (i + 1.5) * 0.5 * (W - 1) - p // W
    dist[:, 2] = dist[:, 1] - H // 2
    c["dist"] = dist
    head = np.arange(P) // HD
    which = np.arange(P) // KEYS
    c["vmask"] = (head[None] % 2 == which[:, None]) * 1.0
    c["rowsum"] = c["vmask"][:, :32]
    c["kmask"] = (head[:, None] % 4 == np.arange(4)[None]) * 1.0
    c["block"] = (head[:, None] == np.arange(8)[None]) * 1.0
    c["half"] = 0.5 * c["block"]
    pick = np.zeros((P, 2, 2, 2, KEYS))
    for q in range(2):
        for i in range(4):
            pick[4 * q + i, q, i // 2, i % 2] = 1
    c["pick"] = pick
    return np.concatenate([c[n].reshape(P, -1) for n in CONST_W], axis=1).astype(np.float32)


def reach(k):
    outs = [o for o in range(HG) if 0 <= R * o + k - PAD < H]
    return outs[0], len(outs), R * outs[0] + k - PAD


ALL_TAPS = sorted(((kh, kw) for kh in range(KS) for kw in range(KS)),
                  key=lambda t: -reach(t[0])[1] * reach(t[1])[1])
PE_TAPS = [(3, 3)] + [t for t in ALL_TAPS[3:] if t != (3, 3)][-21:]
DVE_TAPS = [t for t in ALL_TAPS if t not in PE_TAPS]


def build(nc, x_tok, x_par, x_chan, early, late, rows, const, out):
    with ExitStack() as ctx:
        def sb(name, shape, dt=F32):
            return ctx.enter_context(nc.sbuf_tensor(name, shape, dt))

        def sem(name):
            return ctx.enter_context(nc.semaphore(name))

        xt = sb("xt", [P, TILES, C])
        xp = sb("xp", [P, TILES, C])
        xc = sb("xc", [C, TILES, P])
        ew = sb("ew", [P, EARLY_N])
        lw = sb("lw", [P, LATE_N + P])
        rb = sb("rb", [P, len(ROWS), C])
        cs = sb("cs", [P, CONST_N])
        ones = sb("ones", [P, P])
        negpick = sb("negpick", [8, 4 * P], F32R)
        mhalf = sb("mhalf", [P, TILES])
        stats = sb("stats", [P, TILES, 6])
        mv = sb("mv", [P, TILES, 2])
        vareps = sb("vareps", [P, TILES])
        rstd = sb("rstd", [P, TILES])
        xn = sb("xn", [P, TILES, C])
        xg = sb("xg", [P, TILES, C])
        xl = sb("xl", [P, TILES, C])
        qbias4 = sb("qbias4", [C, 4, P])
        q_img = sb("q_img", [C, H, 2, W // 2, B])
        diag = sb("diag", [C, len(PE_TAPS), P])
        acc = sb("acc", [C, 2, HG, HG * B])
        accs = sb("accs", [C, KEYS * B])
        conv = sb("conv", [C, KEYS, B])
        og = sb("og", [C, B, KEYS])
        pwb = sb("pwb", [C, 2, P])
        th = sb("th", [P, 2, B, KEYS])
        dist = sb("dist", [P, 3, B, KEYS])
        absd = sb("absd", [P, 3, B, KEYS])
        hat = sb("hat", [P, 3, B, KEYS])
        wt = sb("wt", [P, 2, B, KEYS])
        it = sb("it", [C, B, 2, KEYS])
        gmlp = sb("gmlp", [C, C])
        fw = sb("fw", [C, 4, C])
        fb = sb("fb", [C, 4])
        bd1 = sb("bd1", [C, 2, 8, 16])
        ab = sb("ab", [C, 4, 16])
        abd = sb("abd", [C, 4, 8, 16])
        m1 = sb("m1", [C, C])
        fl = sb("fl", [C, 4, C])
        nw1 = sb("nw1", [C, C])
        row_bc = sb("row_bc", [P, C])
        mlp_row = sb("mlp_row", [P, C])
        rowc = sb("rowc", [C, 1])
        kbm = sb("kbm", [C, 4])
        qh = sb("qh", [C, B, 2, P])
        qhr = sb("qhr", [C, B, 2, P], F32R)
        kbd = sb("kbd", [C, B, 4, KEYS])
        kbr = sb("kbr", [C, B, 4, KEYS], F32R)
        vbd = sb("vbd", [P, B, C])
        mx = sb("mx", [P, 2, 2, 2, 4])
        pt = sb("pt", [P, 2, 4, 2 * P])
        rs = sb("rs", [C, 2, 2 * P])
        at = sb("at", [C, 2, 2, P])
        mxt = sb("mxt", [8, 2, 2, P], F32R)
        z = sb("z", [P, TILES, C])
        stats2 = sb("stats2", [P, TILES, 6])
        mv2 = sb("mv2", [P, TILES, 2])
        vareps2 = sb("vareps2", [P, TILES])
        rstd2 = sb("rstd2", [P, TILES])
        u = sb("u", [P, TILES, C])
        ug = sb("ug", [P, TILES, C])
        x1 = sb("x1", [P, TILES, C])
        ct = sb("ct", [C, 2, 2, 2, P])
        o1k = sb("o1k", [C, 2, 2, 2, P])
        o1n = sb("o1n", [C, 2, 2, 2, P])
        yc = sb("yc", [C, 2, 2, 2, P])
        ys = sb("ys", [C, 2, 2, 2, P])
        yd = sb("yd", [P, 2, 2, 2, C])
        lim = sb("lim", [C, 2])
        fin = sb("fin", [P, TILES, C])

        bank = [ctx.enter_context(nc.psum_tensor(f"bank{i}", [P, 512], F32)) for i in range(8)]
        ps_s = bank[0:2]
        ps_t = bank[2:4]
        ps_av = bank[4]
        ps_out = bank[5]
        ps_mix = bank[6:8]

        def const_ap(name):
            return cs[:, CONST[name][0]:CONST[name][1]]

        def late_ap(name):
            return lw[:, LATE[name][0]:LATE[name][1]]

        def vec(name):
            i = P + NTAP + VEC[name]
            return ew[:, i:i + 1]

        wq = ew[:, 0:P]
        ident, cas = const_ap("ident"), const_ap("cas")
        wsd = const_ap("wsd").rearrange("p (a n) -> p a n", a=2)
        winv = const_ap("winv").rearrange("p (a n) -> p a n", a=2)
        dconst = const_ap("dist").rearrange("p (a n) -> p a n", a=3)
        kmask = const_ap("kmask")
        block8, half8 = const_ap("block"), const_ap("half")
        mo_g = lw[:, LATE["mo"][0]:LATE["mo"][0] + 2 * P]
        wqq, wvk, wvv, wmlp = (fw[:, i, :] for i in range(4))
        w0, w1, wk, wn = (fl[:, i, :] for i in range(4))

        d_x, d_early, d_rows, d_ident, d_const, d_late, d_xp, d_xc, d_out = (
            sem("d_" + n) for n in ("x0", "early", "rows", "ident", "const", "late", "xp", "xc", "out"))
        d_x = [d_x, sem("d_x1")]
        s_ones, s_mhalf = sem("s_ones"), sem("s_mhalf")
        s_stats, s_mv, s_var, s_rstd = sem("s_stats"), sem("s_mv"), sem("s_var"), sem("s_rstd")
        s_xn, s_xg, s_xl = sem("s_xn"), sem("s_xg"), sem("s_xl")
        s_colsum, s_qbias, s_qps, s_qimg = sem("s_colsum"), sem("s_qbias"), sem("s_qps"), sem("s_qimg")
        s_diag, s_acc, s_accs = sem("s_diag"), [sem("s_acc0"), sem("s_acc1")], sem("s_accs")
        s_convps, s_conv, s_og = sem("s_convps"), sem("s_conv"), sem("s_og")
        s_pwb, s_gmlp, s_bd1, s_ab, s_abd = (sem("s_" + n) for n in ("pwb", "gmlp", "bd1", "ab", "abd"))
        s_fwps, s_fw, s_fbps, s_fb, s_m1 = (sem("s_" + n) for n in ("fwps", "fw", "fbps", "fb", "m1"))
        s_gps, s_g, s_rowbc, s_flps, s_fl = (sem("s_" + n) for n in ("gps", "g", "rowbc", "flps", "fl"))
        s_xp, s_xc, s_lim, s_kbm, s_negid = (sem("s_" + n) for n in ("xp", "xc", "lim", "kbm", "negid"))
        s_qhps, s_qh, s_qhr = sem("s_qhps"), sem("s_qh"), sem("s_qhr")
        s_off, s_th, s_dist, s_abs, s_hat, s_wt = (
            sem("s_" + n) for n in ("off", "th", "dist", "abs", "hat", "wt"))
        s_itps, s_it, s_kps, s_kbd, s_kbr, s_vps, s_vbd = (
            sem("s_" + n) for n in ("itps", "it", "kps", "kbd", "kbr", "vps", "vbd"))
        s_mxtps, s_mxt = sem("s_mxtps"), sem("s_mxt")
        s_s, s_mx, s_st, s_exp, s_av, s_rs, s_at = (
            sem("s_" + n) for n in ("s", "mx", "st", "exp", "av", "rs", "at"))
        s_out, s_z, s_stats2, s_mv2, s_var2, s_rstd2, s_u, s_ug, s_x1 = (
            sem("s_" + n) for n in ("out", "z", "stats2", "mv2", "var2", "rstd2", "u", "ug", "x1"))
        s_ctps, s_ct, s_tps, s_o1k, s_o1n, s_yps, s_yc, s_ys, s_ydps, s_yd, s_fps, s_fin = (
            [sem(f"s_{n}{par}") for par in range(2)]
            for n in ("ctps", "ct", "tps", "o1k", "o1n", "yps", "yc", "ys", "ydps", "yd", "fps", "fin"))

        def window(kh, kw):
            oh, nh, ih = reach(kh)
            ow, nw, iw = reach(kw)
            src = q_img[:, ih:ih + R * nh - 1:R, iw % 2, iw // 2:iw // 2 + nw, :].rearrange("c h w b -> c h (w b)")
            return src, slice(oh, oh + nh), slice(B * ow, B * (ow + nw))

        def tap(kh, kw):
            i = P + kh * KS + kw
            return ew[:, i:i + 1]

        block = ctx.enter_context(nc.Block())

        @block.sync
        def _(sp):
            for g in range(2):
                sp.dma_start(xt[:, 4 * g:4 * g + 4, :], x_tok[:, 4 * g:4 * g + 4, :]).then_inc(d_x[g], 16)
            sp.dma_start(rb[:].rearrange("p a n -> p (a n)"), rows.broadcast_to([P, len(ROWS) * C])).then_inc(d_rows, 16)
            sp.dma_start(lw[:, 0:LATE_N], late).then_inc(d_late, 16)
            sp.dma_start(xc[:], x_chan).then_inc(d_xc, 16)
            sp.dma_start(xp[:], x_par).then_inc(d_xp, 16)
            for g in range(2):
                for par in range(2):
                    sp.wait_ge(s_fin[par], g + 1)
                    sp.dma_start(out[:, 4 * g + par:4 * g + par + 3:2, :],
                                 fin[:, 4 * g + par:4 * g + par + 3:2, :]).then_inc(d_out, 16)
            sp.wait_ge(d_out, 64)

        @block.gpsimd
        def _(pool):
            pool.memset(ones[:], 1.0).then_inc(s_ones, 1)
            pool.memset(mhalf[:], -0.5).then_inc(s_mhalf, 1)
            pool.wait_ge(s_mhalf, 1)
            for g in range(2):
                pool.wait_ge(s_var, g + 1)
                pool.tensor_tensor(rstd[:, 4 * g:4 * g + 4], vareps[:, 4 * g:4 * g + 4],
                                   mhalf[:, 4 * g:4 * g + 4], ALU.pow).then_inc(s_rstd, 1)
            pool.wait_ge(d_rows, 16)
            for g in range(2):
                pool.wait_ge(s_xn, 4 * g + 4)
                t = slice(4 * g, 4 * g + 4)
                pool.tensor_tensor(xg[:, t, :], xn[:, t, :], rb[:, 0:1, :].broadcast_to([P, 4, C]),
                                   ALU.mult).then_inc(s_xg, 1)
                pool.wait_ge(s_xg, g + 1)
                pool.tensor_tensor(xl[:, t, :], xg[:, t, :], rb[:, 1:2, :].broadcast_to([P, 4, C]),
                                   ALU.add).then_inc(s_xl, 1)
            pool.wait_ge(d_late, 16)
            pool.wait_ge(d_early, 16)
            pool.tensor_tensor(gmlp[:], late_ap("mlp"), vec("ln_g").broadcast_to([C, C]), ALU.mult).then_inc(s_gmlp, 1)
            for k in range(2):
                pool.tensor_copy(pwb[:, k, :], vec(f"pw{k}").broadcast_to([C, P])).then_inc(s_pwb, 1)
            for i, name in enumerate(("w2", "w2T")):
                a = lw[:, LATE[name][0]:LATE[name][0] + 16]
                b = lw[:, LATE[name][0] + 16:LATE[name][1]]
                pool.tensor_tensor(ab[:, 2 * i, :], a, b, ALU.add).then_inc(s_ab, 1)
                pool.tensor_tensor(ab[:, 2 * i + 1, :], a, b, ALU.subtract).then_inc(s_ab, 1)
            pool.wait_ge(d_const, 16)
            for i in range(2):
                w = lw[:, LATE["w1"][0] + 16 * i:LATE["w1"][0] + 16 * i + 16]
                pool.tensor_tensor(bd1[:, i], w.unsqueeze(1).broadcast_to([C, 8, 16]),
                                   block8.unsqueeze(2).broadcast_to([C, 8, 16]), ALU.mult).then_inc(s_bd1, 1)
            pool.wait_ge(s_ab, 4)
            for i in range(4):
                pool.tensor_tensor(abd[:, i], ab[:, i, :].unsqueeze(1).broadcast_to([C, 8, 16]),
                                   half8.unsqueeze(2).broadcast_to([C, 8, 16]), ALU.mult).then_inc(s_abd, 1)
            pool.wait_ge(s_abd, 4)
            pool.wait_ge(d_ident, 16)
            pool.tensor_tensor(m1[:], ident, abd[:, 1].rearrange("p a n -> p (a n)"), ALU.add).then_inc(s_m1, 1)
            pool.wait_ge(d_xp, 16)
            pool.wait_ge(s_rowbc, 1)
            for g in range(2):
                t = slice(4 * g, 4 * g + 4)
                pool.tensor_tensor(xp[:, t, :], xp[:, t, :], row_bc[:].unsqueeze(1).broadcast_to([P, 4, C]),
                                   ALU.add).then_inc(s_xp, 1)
            for b in range(B):
                pool.wait_ge(s_var2, b + 1)
                pool.tensor_tensor(rstd2[:, 2 * b:2 * b + 2], vareps2[:, 2 * b:2 * b + 2],
                                   mhalf[:, 0:2], ALU.pow).then_inc(s_rstd2, 1)

        @block.scalar
        def _(act):
            act.dma_start(ew[:], early).then_inc(d_early, 16)
            act.dma_start(cs[:, 0:P], const[:, 0:P]).then_inc(d_ident, 16)
            act.dma_start(cs[:, P:CONST_N], const[:, P:CONST_N]).then_inc(d_const, 16)
            act.wait_ge(d_early, 16)
            act.wait_ge(d_ident, 16)
            for n, (kh, kw) in enumerate(PE_TAPS):
                act.activation(diag[:, n, :], ident, ACT.Copy, scale=tap(kh, kw)).then_inc(s_diag, 1)
            act.wait_ge(d_const, 16)
            act.mul(negpick[:], const_ap("pick")[0:8], -1.0).then_inc(s_negid, 1)
            act.wait_ge(s_fwps, 1)
            act.copy(fw[:], ps_mix[0][:].rearrange("p (a n) -> p a n", a=4)).then_inc(s_fw, 1)
            act.wait_ge(s_fb, 1)
            for g in range(2):
                act.wait_ge(s_qhps, g + 1)
                src = (ps_av, ps_out)[g][:].rearrange("p (b a n) -> p b a n", b=2, a=2)
                act.activation(qh[:, 2 * g:2 * g + 2], src, ACT.Identity, bias=fb[:, 0:1]).then_inc(s_qh, 1)
                act.activation(qhr[:, 2 * g:2 * g + 2], src, ACT.Identity, bias=fb[:, 0:1]).then_inc(s_qhr, 1)
            act.wait_ge(s_conv, 1)
            act.activation(og[:], conv[:].rearrange("c n b -> c b n"), ACT.Gelu, bias=vec("dw_b")).then_inc(s_og, 1)
            act.wait_ge(s_off, 1)
            for k in (1, 0):
                act.activation(th[:, k], ps_t[0][:, 256 * k:256 * k + 256].rearrange("p (b n) -> p b n", b=B),
                               ACT.Tanh).then_inc(s_th, 1)
            for i in range(3):
                act.wait_ge(s_dist, i + 1)
                act.activation(absd[:, i], dist[:, i], ACT.Abs).then_inc(s_abs, 1)
            act.wait_ge(s_gps, 1)
            act.copy(lw[:, LATE_N:LATE_N + P], ps_out[:, 0:P]).then_inc(s_g, 1)
            act.wait_ge(s_flps, 1)
            act.copy(fl[:], ps_mix[1][:].rearrange("p (a n) -> p a n", a=4)).then_inc(s_fl, 1)
            act.mul(nw1[:], ps_mix[1][:, P:2 * P], -1.0).then_inc(s_fl, 1)
            act.wait_ge(s_itps, 1)
            for i in range(2):
                act.copy(it[:, :, i, :], ps_mix[0][:, 0:256].rearrange("p (b n) -> p b n", b=B)).then_inc(s_it, 1)
            act.wait_ge(s_kps, 1)
            act.wait_ge(s_kbm, 1)
            kps = ps_out[:, 0:256].rearrange("p (b n) -> p b n", b=B)
            for i in range(4):
                act.activation(kbr[:, :, i, :], kps, ACT.Identity, bias=kbm[:, i:i + 1],
                               scale=kmask[:, i:i + 1]).then_inc(s_kbr, 1)

            def exp(b):
                if b >= 2:
                    act.wait_ge(s_av, b - 1)
                for a in range(2):
                    act.wait_ge(s_st, 2 * b + a + 1)
                    act.activation(pt[:, b % 2, 2 * a:2 * a + 2, :],
                                   ps_t[a][:].rearrange("p (i n) -> p i n", i=2), ACT.Exp).then_inc(s_exp, 1)

            def gelu(b):
                act.wait_ge(s_u, 2 * b + 2)
                t = slice(2 * b, 2 * b + 2)
                act.activation(ug[:, t, :], u[:, t, :], ACT.Gelu).then_inc(s_ug, 1)

            def sums(g, par):
                act.wait_ge(s_ctps[par], g + 1)
                act.copy(ct[:, g, par], ps_mix[par][:, 0:256].rearrange("p (b n) -> p b n", b=2)
                         ).then_inc(s_ct[par], 1)

            def relu_k(g, par):
                act.wait_ge(s_tps[par], g + 1)
                act.activation(o1k[:, g, par], ps_mix[par][:, 256:512].rearrange("p (b n) -> p b n", b=2),
                               ACT.Relu, bias=vec("b1k")).then_inc(s_o1k[par], 1)

            def back(g, par):
                act.wait_ge(s_ydps[par], g + 1)
                act.copy(yd[:, g, par], ps_mix[par][:, 256:512].rearrange("p (b n) -> p b n", b=2)
                         ).then_inc(s_yd[par], 1)

            exp(0)
            exp(1)
            exp(2)
            gelu(0)
            gelu(1)
            sums(0, 0)
            sums(0, 1)
            exp(3)
            for step in (relu_k, back):
                for par in range(2):
                    step(0, par)
            gelu(2)
            gelu(3)
            for step in (sums, relu_k, back):
                for par in range(2):
                    step(1, par)

        @block.vector
        def _(dve):
            for g in range(2):
                dve.wait_ge(d_x[g], 16)
                for i in range(4 * g, 4 * g + 4):
                    dve.bn_stats(stats[:, i, :], xt[:, i, :]).then_inc(s_stats, 1)
                for i in range(4 * g, 4 * g + 4):
                    dve.wait_ge(s_stats, i + 1)
                    dve.bn_aggr(mv[:, i, :], stats[:, i, :]).then_inc(s_mv, 1)
                dve.wait_ge(s_mv, 4 * g + 4)
                dve.tensor_scalar(vareps[:, 4 * g:4 * g + 4], mv[:, 4 * g:4 * g + 4, 1], EPS, None,
                                  ALU.add).then_inc(s_var, 1)
            for g in range(2):
                dve.wait_ge(s_rstd, g + 1)
                for i in range(4 * g, 4 * g + 4):
                    dve.tensor_scalar(xn[:, i, :], xt[:, i, :], mv[:, i, 0:1], rstd[:, i:i + 1],
                                      ALU.subtract, ALU.mult).then_inc(s_xn, 1)
            dve.wait_ge(s_colsum, 1)
            dve.wait_ge(d_rows, 16)
            dve.wait_ge(d_early, 16)
            for i in range(4):
                dve.scalar_tensor_tensor(out=qbias4[:, i, :], in0=ps_t[0][:, 0:P], scalar=vec("ln_b"),
                                         in1=rb[:, 2, :], op0=ALU.mult, op1=ALU.add).then_inc(s_qbias, 1)
            dve.wait_ge(s_qbias, 4)
            for g in range(2):
                dve.wait_ge(s_qps, g + 1)
                dve.scalar_tensor_tensor(
                    out=q_img[:, :, :, :, 2 * g:2 * g + 2].rearrange("c h p w b -> c b (h p w)"),
                    in0=ps_s[g][:].rearrange("c (b n) -> c b n", b=2), scalar=vec("ln_g"),
                    in1=qbias4[:].rearrange("c (b a) n -> c b (a n)", b=2),
                    op0=ALU.mult, op1=ALU.add).then_inc(s_qimg, 1)
            dve.wait_ge(s_qimg, 2)
            for n, (kh, kw) in enumerate(DVE_TAPS):
                src, oh, ow = window(kh, kw)
                a = n % 2
                if n < 2:
                    dve.tensor_scalar(acc[:, a], src, tap(kh, kw), None, ALU.mult).then_inc(s_acc[a], 1)
                    continue
                dst = acc[:, a, oh, ow]
                dve.wait_ge(s_acc[a], n // 2)
                dve.scalar_tensor_tensor(out=dst, in0=src, scalar=tap(kh, kw), in1=dst, op0=ALU.mult,
                                         op1=ALU.add).then_inc(s_acc[a], 1)
            dve.wait_ge(s_acc[0], (len(DVE_TAPS) + 1) // 2)
            dve.wait_ge(s_acc[1], len(DVE_TAPS) // 2)
            dve.tensor_tensor(accs[:], acc[:, 0].rearrange("c h w -> c (h w)"),
                              acc[:, 1].rearrange("c h w -> c (h w)"), ALU.add).then_inc(s_accs, 1)
            dve.wait_ge(s_accs, 1)
            dve.wait_ge(s_convps, 1)
            dve.tensor_tensor(conv[:].rearrange("c n b -> c (n b)"), ps_t[1][:, 0:256], accs[:], ALU.add).then_inc(s_conv, 1)
            dve.wait_ge(s_fbps, 1)
            i = P + NTAP + VEC["mq_b"]
            dve.tensor_tensor(fb[:], ps_mix[1][:, 0:4], ew[:, i:i + 4], ALU.add).then_inc(s_fb, 1)
            dve.wait_ge(s_fb, 1)
            dve.tensor_scalar(kbm[:], kmask, fb[:, 1:2], None, ALU.mult).then_inc(s_kbm, 1)
            dve.tensor_scalar(lim[:, 0:1], fb[:, 3:4], -1.0, -SPARSITY, ALU.mult, ALU.add).then_inc(s_lim, 1)
            dve.tensor_scalar(lim[:, 1:2], fb[:, 3:4], -1.0, SPARSITY, ALU.mult, ALU.add).then_inc(s_lim, 1)
            for i, k in enumerate((1, 0, 0)):
                dve.wait_ge(s_th, 1 if k == 1 else 2)
                dve.scalar_tensor_tensor(out=dist[:, i], in0=th[:, k], scalar=COORD,
                                         in1=dconst[:, i:i + 1, :].broadcast_to([P, B, KEYS]),
                                         op0=ALU.mult, op1=ALU.add).then_inc(s_dist, 1)
            for i in range(3):
                dve.wait_ge(s_abs, i + 1)
                dve.tensor_scalar(hat[:, i], absd[:, i], -1.0, 0.0, ALU.add, ALU.min).then_inc(s_hat, 1)
            for i in range(2):
                dve.wait_ge(s_hat, i + 2)
                dve.tensor_tensor(wt[:, i], hat[:, 0], hat[:, 1 + i], ALU.mult).then_inc(s_wt, 1)
            dve.wait_ge(s_gps, 1)
            dve.wait_ge(s_g, 1)
            dve.tensor_tensor(row_bc[:], ps_out[:, P:2 * P], rb[:, 3, :], ALU.add).then_inc(s_rowbc, 1)
            dve.tensor_tensor(mlp_row[:], ps_out[:, 2 * P:3 * P], rb[:, 4, :], ALU.add).then_inc(s_rowbc, 1)
            dve.tensor_tensor(rowc[:], ps_out[:, 3 * P:3 * P + 1], vec("mo_b"), ALU.add).then_inc(s_rowbc, 1)
            dve.wait_ge(s_kps, 1)
            kps = ps_av[:, 0:256].rearrange("p (b n) -> p b n", b=B)
            for i in range(4):
                dve.tensor_scalar(kbd[:, :, i, :], kps, fb[:, 1:2], kmask[:, i:i + 1], ALU.add,
                                  ALU.mult).then_inc(s_kbd, 1)
            dve.wait_ge(s_vps, 1)
            dve.tensor_tensor(vbd[:], ps_mix[1][:].rearrange("p (b n) -> p b n", b=B),
                              const_ap("vmask").unsqueeze(1).broadcast_to([P, B, C]), ALU.mult).then_inc(s_vbd, 1)
            dve.wait_ge(d_xc, 16)
            dve.wait_ge(s_rowbc, 3)
            dve.tensor_scalar(xc[:], xc[:], rowc[:, 0:1], None, ALU.add).then_inc(s_xc, 1)

            def row_max(b):
                if b >= 2:
                    dve.wait_ge(s_mxtps, 2 * b - 2)
                for a in range(2):
                    dve.wait_ge(s_s, 2 * b + a + 1)
                    dve.tensor_reduce(mx[:, b % 2, a], ps_s[a][:].rearrange("p (q i n) -> p q i n", q=2, n=KEYS),
                                      AX_X, ALU.max).then_inc(s_mx, 1)

            def turned_max(b):
                if b >= 2:
                    dve.wait_ge(s_st, 2 * b - 2)
                for a in range(2):
                    dve.wait_ge(s_mxtps, 2 * b + a + 1)
                    dve.tensor_copy(mxt[:, b % 2, a], ps_s[a][0:8, 0:P]).then_inc(s_mxt, 1)

            def divide(b):
                dve.wait_ge(s_av, b + 1)
                if b >= 2:
                    dve.wait_ge(s_at, b - 1)
                    dve.wait_ge(s_out, b - 1)
                dve.reciprocal(rs[:, b % 2], ps_av[:, 256:512]).then_inc(s_rs, 1)
                dve.wait_ge(s_rs, b + 1)
                dve.tensor_tensor(at[:, b % 2].rearrange("c a n -> c (a n)"), ps_av[:, 0:256],
                                  rs[:, b % 2], ALU.mult).then_inc(s_at, 1)

            def residual(b):
                t = slice(2 * b, 2 * b + 2)
                dve.wait_ge(s_out, b + 1)
                dve.wait_ge(s_xp, b // 2 + 1)
                dve.tensor_tensor(z[:, t, :], ps_out[:].rearrange("p (i n) -> p i n", i=2)[:, :, 0:C],
                                  xp[:, t, :], ALU.add).then_inc(s_z, 1)
                dve.wait_ge(s_z, b + 1)
                for i in (2 * b, 2 * b + 1):
                    dve.bn_stats(stats2[:, i, :], z[:, i, :]).then_inc(s_stats2, 1)
                for i in (2 * b, 2 * b + 1):
                    dve.wait_ge(s_stats2, i + 1)
                    dve.bn_aggr(mv2[:, i, :], stats2[:, i, :]).then_inc(s_mv2, 1)
                dve.wait_ge(s_mv2, 2 * b + 2)
                dve.tensor_scalar(vareps2[:, t], mv2[:, t, 1], EPS, None, ALU.add).then_inc(s_var2, 1)

            def mlp_in(b):
                dve.wait_ge(s_rstd2, b + 1)
                for i in range(2):
                    dve.scalar_tensor_tensor(out=u[:, 2 * b + i, :], in0=ps_out[:, 256 * i + C:256 * i + 2 * C],
                                             scalar=rstd2[:, 2 * b + i:2 * b + i + 1], in1=mlp_row[:],
                                             op0=ALU.mult, op1=ALU.add).then_inc(s_u, 1)

            def block_out(b):
                t = slice(2 * b, 2 * b + 2)
                dve.wait_ge(s_ug, b + 1)
                dve.tensor_tensor(x1[:, t, :], ug[:, t, :], z[:, t, :], ALU.add).then_inc(s_x1, 1)

            def relu_n(g, par):
                dve.wait_ge(s_tps[par], g + 1)
                dve.wait_ge(s_o1k[par], g + 1)
                dve.tensor_scalar(o1n[:, g, par], ps_mix[par][:, 256:512].rearrange("p (b n) -> p b n", b=2),
                                  vec("b1n"), 0.0, ALU.add, ALU.max).then_inc(s_o1n[par], 1)

            def threshold(g, par):
                y = ps_mix[par][:, 0:256].rearrange("p (b n) -> p b n", b=2)
                dve.wait_ge(s_yps[par], g + 1)
                dve.tensor_scalar(yc[:, g, par], y, lim[:, 0:1], lim[:, 1:2], ALU.max, ALU.min
                                  ).then_inc(s_yc[par], 1)
                dve.wait_ge(s_yc[par], g + 1)
                dve.tensor_tensor(ys[:, g, par], y, yc[:, g, par], ALU.subtract).then_inc(s_ys[par], 1)

            def finish(g, par):
                dve.wait_ge(s_fps[par], g + 1)
                t = slice(4 * g + par, 4 * g + par + 3, 2)
                dve.tensor_tensor(fin[:, t, :], ps_mix[par][:, 0:256].rearrange("p (b n) -> p b n", b=2),
                                  x1[:, t, :], ALU.add).then_inc(s_fin[par], 1)

            dve.wait_ge(s_lim, 2)
            row_max(0)
            turned_max(0)
            divide(0)
            row_max(1)
            turned_max(1)
            residual(0)
            divide(1)
            mlp_in(0)
            row_max(2)
            turned_max(2)
            residual(1)
            mlp_in(1)
            row_max(3)
            turned_max(3)
            block_out(0)
            block_out(1)
            divide(2)
            relu_n(0, 0)
            residual(2)
            relu_n(0, 1)
            mlp_in(2)
            divide(3)
            threshold(0, 0)
            threshold(0, 1)
            residual(3)
            mlp_in(3)
            finish(0, 0)
            finish(0, 1)
            block_out(2)
            block_out(3)
            for step in (relu_n, threshold, finish):
                for par in range(2):
                    step(1, par)

        @block.tensor
        def _(pe):
            def mm(o, lhsT, rhs, start=True, stop=True):
                return pe.matmul(o, lhsT, rhs, start=start, stop=stop, skip_group_check=True)

            pe.wait_ge(s_ones, 1)
            pe.wait_ge(d_early, 16)
            mm(ps_t[0][:, 0:P], ones[:], wq).then_inc(s_colsum, 1)
            for g in range(2):
                for i in range(4):
                    pe.wait_ge(s_xn, 4 * g + i + 1)
                    last = mm(ps_s[g][:, P * i:P * i + P], xn[:, 4 * g + i, :], wq, start=(i == 0))
                last.then_inc(s_qps, 1)
            pe.wait_ge(d_late, 16)
            pe.wait_ge(d_const, 16)
            mm(ps_mix[0][:, 0:P], late_ap("wqT"), late_ap("mq"))
            mm(ps_mix[0][:, P:2 * P], late_ap("wvT"), late_ap("mk"), start=False)
            mm(ps_mix[0][:, 2 * P:3 * P], late_ap("wvT"), late_ap("mv"), start=False)
            pe.wait_ge(s_gmlp, 1)
            mm(ps_mix[0][:, 3 * P:4 * P], const_ap("center"), gmlp[:], start=False).then_inc(s_fwps, 1)
            pe.wait_ge(s_m1, 1)
            mm(ps_mix[1][:, 0:1], late_ap("mq"), vec("bq"))
            mm(ps_mix[1][:, 1:2], late_ap("mk"), vec("bv"), start=False)
            mm(ps_mix[1][:, 2:3], late_ap("mv"), vec("bv"), start=False)
            mm(ps_mix[1][:, 3:4], m1[:], vec("b2k"), start=False).then_inc(s_fbps, 1)
            pe.wait_ge(s_qimg, 2)
            cps = ps_t[1][:, 0:256].rearrange("c (h w) -> c h w", h=HG)
            for n, (kh, kw) in enumerate(PE_TAPS):
                src, oh, ow = window(kh, kw)
                pe.wait_ge(s_diag, n + 1)
                last = mm(cps[:, oh, ow], diag[:, n, :], src, start=(n == 0), stop=(n == len(PE_TAPS) - 1))
            last.then_inc(s_convps, 1)
            pe.wait_ge(s_fw, 1)
            for g in range(2):
                pe.wait_ge(s_xl, g + 1)
                for i in range(4):
                    o = (ps_av, ps_out)[g][:, 256 * (i // 2):256 * (i // 2) + 256]
                    last = mm(o.rearrange("p (a m) -> p a m", a=2)[:, :, 64 * (i % 2):64 * (i % 2) + 64], wqq,
                              xl[:, 4 * g + i, :].rearrange("p (h a w) -> p a h w", a=2, w=8), start=(i == 0))
                last.then_inc(s_qhps, 1)
            pe.wait_ge(s_bd1, 2)
            pe.wait_ge(s_abd, 4)
            pe.wait_ge(s_fb, 1)
            for i in range(2):
                mm(ps_mix[1][:, P * i:P * i + P], cas, bd1[:, i].rearrange("p a n -> p (a n)"), start=(i == 0))
            at_, bt_ = (abd[:, i].rearrange("p a n -> p (a n)") for i in (2, 3))
            mm(ps_mix[1][:, 2 * P:3 * P], at_, m1[:], start=False)
            mm(ps_mix[1][:, 3 * P:4 * P], bt_, m1[:], start=False, stop=False)
            mm(ps_mix[1][:, 3 * P:4 * P], at_, ident, start=False).then_inc(s_flps, 1)
            pe.wait_ge(s_pwb, 2)
            pe.wait_ge(s_og, 1)
            pe.wait_ge(s_qbias, 4)
            for k in (1, 0):
                last = mm(ps_t[0][:, 256 * k:256 * k + 256], pwb[:, k, :], og[:].rearrange("c b n -> c (b n)"), start=(k == 1))
            last.then_inc(s_off, 1)
            pe.wait_ge(s_qhr, 2)
            mm(ps_out[:, 0:P], late_ap("moT"), wmlp)
            mm(ps_out[:, P:2 * P], fb[:, 2:3].broadcast_to([C, P]), late_ap("mo"), start=False)
            mm(ps_out[:, 2 * P:3 * P], vec("ln_b").broadcast_to([C, P]), late_ap("mlp"), start=False)
            mm(ps_out[:, 3 * P:3 * P + 1], late_ap("mo"), fb[:, 2:3], start=False).then_inc(s_gps, 1)
            pe.wait_ge(s_wt, 2)
            for b in range(B):
                for i in range(2):
                    for c in range(2):
                        last = pe.matmul(ps_mix[0][KEYS * c:KEYS * c + KEYS, KEYS * b:KEYS * b + KEYS],
                                         wt[:, i, b, :], xt[:, 2 * b + i, c:C:2], start=(b == 0 and i == 0),
                                         stop=(i == 1), skip_group_check=True, tile_position=(0, KEYS * c))
            last.then_inc(s_itps, 1)
            pe.wait_ge(s_it, 1)
            mm(ps_av[:, 0:256], wvk, it[:, :, 0, :])
            pe.wait_ge(s_rowbc, 3)
            mm(ps_out[:, 0:256], wvk, it[:, :, 0, :]).then_inc(s_kps, 1)
            pe.wait_ge(s_it, 2)
            pe.wait_ge(s_fl, 2)
            for b in range(B):
                last = mm(ps_mix[1][:, P * b:P * b + P], it[:, b].rearrange("c i n -> c (i n)"), wvv,
                          start=(b == 0))
            last.then_inc(s_vps, 1)

            def scores_q(b):
                if b == 0:
                    pe.wait_ge(s_kbr, 4)
                else:
                    pe.wait_ge(s_mxt, 2 * b)
                for a in range(2):
                    r = slice(64 * a, 64 * a + 64)
                    for q in range(2):
                        last = mm(ps_s[a][:, 256 * q:256 * q + 256], qhr[r, b, q, :],
                                  kbr[r, b].rearrange("c i n -> c (i n)"), start=(q == 0))
                    last.then_inc(s_s, 1)

            def scores_k(b):
                if b == 0:
                    pe.wait_ge(s_kbd, 4)
                for a in range(2):
                    if b >= 1:
                        pe.wait_ge(s_exp, 2 * b - 1 + a)
                    r = slice(64 * a, 64 * a + 64)
                    for i in range(2):
                        mm(ps_t[a][:, 256 * i:256 * i + 256],
                           kbd[r, b, 2 * i:2 * i + 2].rearrange("c i n -> c (i n)"),
                           qh[r, b].rearrange("c a n -> c (a n)"), start=(i == 0), stop=False)

            def turn_max(b):
                for a in range(2):
                    pe.wait_ge(s_mx, 2 * b + a + 1)
                    pe.transpose(ps_s[a][0:8, 0:P], mx[:, b % 2, a].rearrange("p q i -> p (q i)"),
                                 ident).then_inc(s_mxtps, 1)

            def shift(b):
                if b == 0:
                    pe.wait_ge(s_negid, 1)
                for a in range(2):
                    pe.wait_ge(s_mxt, 2 * b + a + 1)
                    for i in range(2):
                        for q in range(2):
                            n = P * (2 * q + i)
                            last = mm(ps_t[a][:, 256 * i + P * q:256 * i + P * q + P], negpick[:, n:n + P],
                                      mxt[:, b % 2, a, :], start=False)
                    last.then_inc(s_st, 1)

            def values(b):
                if b == 0:
                    pe.wait_ge(s_vbd, 1)
                    pe.wait_ge(s_kbd, 4)
                else:
                    pe.wait_ge(s_at, b)
                pe.wait_ge(s_exp, 2 * b + 2)
                for o, rhs in ((0, None), (256, const_ap("rowsum"))):
                    for i in range(4):
                        lhsT = rhs if rhs is not None else vbd[:, b, 32 * i:32 * i + 32]
                        last = pe.matmul(ps_av[32 * i:32 * i + 32, o:o + 256], lhsT, pt[:, b % 2, i, :],
                                         start=(o == 0), stop=True, skip_group_check=True,
                                         tile_position=(0, 32 * i))
                last.then_inc(s_av, 1)

            def outs(b):
                pe.wait_ge(s_at, b + 1)
                if b == 0:
                    pe.wait_ge(s_g, 1)
                    pe.wait_ge(s_rowbc, 3)
                    pe.wait_ge(s_xc, 1)
                else:
                    pe.wait_ge(s_u, 2 * b)
                for par in range(2):
                    mm(ps_out[:, 256 * par:256 * par + 256], at[:, b % 2, par], mo_g, start=(par == 0), stop=False)
                    last = mm(ps_out[:, 256 * par + C:256 * par + 2 * C], xc[:, 2 * b + par, :], wmlp, start=False)
                last.then_inc(s_out, 1)

            def sums(g, par):
                if g == 0 and par == 0:
                    pe.wait_ge(s_it, 2)
                if g == 0 and par == 1:
                    pe.wait_ge(s_vbd, 1)
                if g == 1:
                    pe.wait_ge(s_fin[par], 1)
                for b in range(2):
                    pe.wait_ge(s_x1, 2 * g + b + 1)
                    last = mm(ps_mix[par][:, P * b:P * b + P], x1[:, 4 * g + 2 * b + par, :], wsd[:, par, :],
                              start=(b == 0))
                last.then_inc(s_ctps[par], 1)

            def layer1(g, par):
                pe.wait_ge(s_ct[par], g + 1)
                na, nf = PAIRS[par], FIXED[par]
                o = ps_mix[par][:, 256:512].rearrange("p (b n) -> p b n", b=2)
                src = ct[:, g, par]
                mm(o[:, :, 0:na + nf], w0, src[:, :, 0:na + nf], start=True, stop=False)
                mm(o[:, :, na + nf:P], w0, src[:, :, 0:na], start=False, stop=False)
                mm(o[:, :, 0:na], w1, src[:, :, na + nf:P], start=False)
                mm(o[:, :, na + nf:P], nw1[:], src[:, :, na + nf:P], start=False).then_inc(s_tps[par], 1)

            def layer2(g, par):
                na, nf = PAIRS[par], FIXED[par]
                o = ps_mix[par][:, 0:256].rearrange("p (b n) -> p b n", b=2)
                pe.wait_ge(s_o1k[par], g + 1)
                pe.wait_ge(s_o1n[par], g + 1)
                mm(o, wk, o1k[:, g, par], start=True, stop=False)
                src = o1n[:, g, par]
                if nf:
                    mm(o[:, :, na:na + nf], wn, src[:, :, na:na + nf], start=False)
                mm(o[:, :, 0:na], wn, src[:, :, na + nf:P], start=False)
                mm(o[:, :, na + nf:P], wn, src[:, :, 0:na], start=False).then_inc(s_yps[par], 1)

            def back_c(g, par):
                pe.wait_ge(s_ys[par], g + 1)
                for b in range(2):
                    last = mm(ps_mix[par][:, 256 + P * b:256 + P * b + P], ys[:, g, par, b, :], cas,
                              start=(b == 0))
                last.then_inc(s_ydps[par], 1)

            def back_w(g, par):
                pe.wait_ge(s_yd[par], g + 1)
                mm(ps_mix[par][:, 0:256], winv[:, par, :], yd[:, g, par].rearrange("p b n -> p (b n)")
                   ).then_inc(s_fps[par], 1)

            for b in range(3):
                scores_q(b)
                scores_k(b)
                turn_max(b)
                if b >= 1:
                    outs(b - 1)
                shift(b)
                values(b)
            scores_q(3)
            scores_k(3)
            turn_max(3)
            sums(0, 0)
            sums(0, 1)
            shift(3)
            layer1(0, 0)
            outs(2)
            layer1(0, 1)
            values(3)
            layer2(0, 0)
            layer2(0, 1)
            outs(3)
            back_c(0, 0)
            back_c(0, 1)
            back_w(0, 0)
            back_w(0, 1)
            for step in (sums, layer1, layer2, back_c, back_w):
                for par in range(2):
                    step(1, par)


def lay_out(x, i):
    f = np.ascontiguousarray
    x = np.asarray(x)
    x_tok = f(x.reshape(TILES, P, C).transpose(1, 0, 2))
    xr = x.reshape(B, 8, 2, 8, 2, C)
    x_par = f(xr.transpose(4, 1, 3, 0, 2, 5).reshape(P, TILES, C))
    x_chan = f(xr.transpose(5, 0, 2, 4, 1, 3).reshape(C, TILES, P))
    vecs = {"ln_g": i["L0_conv_ln_g"], "ln_b": i["L0_conv_ln_b"], "dw_b": i["L0_conv_dw_b"],
            "bq": i["L0_conv_bq"], "bv": i["L0_conv_bv"], "mq_b": i["L0_conv_mq_b"],
            "mk_b": i["L0_conv_mk_b"], "mv_b": i["L0_conv_mv_b"], "mo_b": i["L0_conv_mo_b"],
            "mlp_b": i["L0_conv_mlp_b"],
            "b1k": i["L1_conv_b1"][0], "b1n": i["L1_conv_b1"][1], "b2k": i["L1_conv_b2"][0],
            "b2n": i["L1_conv_b2"][1], "pw0": i["L0_conv_pw_w"][0], "pw1": i["L0_conv_pw_w"][1]}
    vecs = {n: np.asarray(v).reshape(C) for n, v in vecs.items()}
    image = lambda a: a.reshape(*a.shape[:-1], 8, 8, 2).swapaxes(-1, -2).reshape(a.shape)
    vecs["bq_img"] = image(vecs["bq"])
    early = np.concatenate([image(i["L0_conv_wq"]), i["L0_conv_dw_w"].reshape(C, NTAP),
                            np.stack([vecs[n] for n in VECTORS], axis=1)], axis=1)
    w1 = i["L1_conv_w1"].transpose(1, 2, 0, 3).reshape(C, 32)
    w2 = i["L1_conv_w2"].transpose(1, 2, 0, 3).reshape(C, 32)
    w2t = i["L1_conv_w2"].transpose(1, 3, 0, 2).reshape(C, 32)
    late = np.concatenate([i["L0_conv_wq"].T, i["L0_conv_mq_w"], i["L0_conv_wv"].T, i["L0_conv_mk_w"],
                           i["L0_conv_mv_w"], i["L0_conv_mo_w"].T, i["L0_conv_mlp_w"], w1, w2, w2t,
                           i["L0_conv_mo_w"]], axis=1)
    rows = np.concatenate([vecs[n] for n in ROWS])[None]
    return {"x_tok": x_tok, "x_par": x_par, "x_chan": x_chan, "early": f(early), "late": f(late),
            "rows": f(rows), "const": constants()}


def kernel(**inputs):
    import concourse.bacc as bacc
    from concourse.bass_utils import run_bass_kernel_spmd as run

    inputs = {n: np.asarray(v) for n, v in inputs.items()}
    arrays = lay_out(inputs["x"], inputs)
    nc = bacc.Bacc("TRN2", target_bir_lowering=False, num_devices=1)
    args = [nc.dram_tensor(f"in_{n}", a.shape, F32, kind="ExternalInput").ap() for n, a in arrays.items()]
    out = nc.dram_tensor("out_tiles", (P, TILES, C), F32, kind="ExternalOutput").ap()
    build(nc, *args, out)
    r = run(nc, [{f"in_{n}": a for n, a in arrays.items()}], core_ids=[0])
    o = np.asarray(r.results[0]["out_tiles"]).reshape(2, 8, 8, B, 2, C)
    return np.ascontiguousarray(o.transpose(3, 1, 4, 2, 0, 5).reshape(B, H, W, C))
```

```python
from contextlib import ExitStack

import numpy as np

import concourse.bass as bass
from concourse import mybir

ALU = mybir.AluOpType
ACT = mybir.ActivationFunctionType
F32 = mybir.dt.float32
F32R = mybir.dt.float32r
AX_X = mybir.AxisListType.X

B, H, W, C = 4, 16, 16, 128
P = 128
HEADS, HD = 8, 16
KS, PAD, R = 7, 3, 2
HG = H // R
KEYS = HG * HG
TILES = B * 2
EPS = 1e-5
SPARSITY = 0.01
COORD = 4.0 * 0.5 * (W - 1)

CONST_W = {"ident": P, "wsd": 2 * P, "winv": 2 * P, "cas": P, "center": P, "dist": 2 * KEYS, "lower": 1,
           "vmask": P, "rowsum": 32, "kmask": 4, "block": 8, "half": 8}
CONST = {}
_at = 0
for _name, _w in CONST_W.items():
    CONST[_name] = (_at, _at + _w)
    _at += _w
CONST_N = _at

VECTORS = ["ln_g", "ln_b", "dw_b", "bq", "bv", "mq_b", "mk_b", "b2n", "mo_b", "b1k", "b1n",
           "b2k", "pw0", "pw1"]
VEC = {n: i for i, n in enumerate(VECTORS)}
NTAP = KS * KS
EARLY_N = P + NTAP + len(VECTORS)
WEIGHTS = ["wqT", "mq", "wvT", "mk", "mv", "moT", "mlp"]
LATE = {n: (i * P, (i + 1) * P) for i, n in enumerate(WEIGHTS)}
_at = len(WEIGHTS) * P
for _name in ("w1", "w2", "w2T"):
    LATE[_name] = (_at, _at + 32)
    _at += 32
LATE["mo"] = (_at, _at + P)
LATE_N = _at + P
ROWS = ["ln_g", "ln_b", "bq_img", "mo_b", "mlp_b", "mv_b"]

def tile_tokens(par):
    return [(2 * h2 + par, 2 * w2 + half) for half in range(2) for h2 in range(8) for w2 in range(8)]


def frequency_pairs(par):
    first, fixed, second, seen = [], [], [], set()
    for h in range(par, H, 2):
        for v in range(W):
            a, b = (h, v), ((-h) % H, (-v) % W)
            if a in seen:
                continue
            seen |= {a, b}
            if a == b:
                fixed.append(a)
            else:
                first.append(a)
                second.append(b)
    return first, fixed, second


PAIRS = [len(frequency_pairs(par)[0]) for par in range(2)]
FIXED = [len(frequency_pairs(par)[1]) for par in range(2)]


def constants():
    c = {}
    eye = np.eye(P)
    c["ident"] = eye

    def cas(n):
        t = np.arange(n)
        a = 2.0 * np.pi * (np.outer(t, t) % n) / n
        return np.cos(a) + np.sin(a)

    cw = cas(W)
    wsd, winv = np.zeros((P, 2, P)), np.zeros((P, 2, P))
    for par in range(2):
        first, fixed, second = frequency_pairs(par)
        for row, (h, w) in enumerate(tile_tokens(par)):
            for n, (fh, fv) in enumerate(first + fixed):
                gh, gv = (-fh) % H, (-fv) % W
                s = cw[fv, w] * (fh == h) + cw[gv, w] * (gh == h)
                d = cw[fv, w] * (fh == h) - cw[gv, w] * (gh == h)
                wsd[row, par, n] = 0.5 * s
                if n < len(first):
                    wsd[row, par, len(first) + len(fixed) + n] = 0.5 * d
            for n, (fh, fv) in enumerate(first + fixed + second):
                winv[n, par, row] = cw[fv, w] * (fh == h) / (W * C)
    c["wsd"], c["winv"], c["cas"] = wsd, winv, cas(C)
    c["center"] = eye - 1.0 / C
    p = np.arange(P)[:, None]
    i, j = np.arange(KEYS)[None] // HG, np.arange(KEYS)[None] % HG
    dist = np.zeros((P, 2, KEYS))
    dist[:, 0] = (j + 1.5) * 0.5 * (W - 1) - p % W
    dist[:, 1] = (i + 1.5) * 0.5 * (W - 1) - p // W
    c["dist"] = dist
    c["lower"] = np.full((P, 1), -(H // 2))
    head = np.arange(P) // HD
    which = np.arange(P) // KEYS
    c["vmask"] = (head[None] % 2 == which[:, None]) * 1.0
    c["rowsum"] = c["vmask"][:, :32]
    c["kmask"] = (head[:, None] % 4 == np.arange(4)[None]) * 1.0
    c["block"] = (head[:, None] == np.arange(8)[None]) * 1.0
    c["half"] = 0.5 * c["block"]
    return np.concatenate([c[n].reshape(P, -1) for n in CONST_W], axis=1).astype(np.float32)


def picks():
    pick = np.zeros((8, 2, 2, 2, KEYS), np.float32)
    for q in range(2):
        for i in range(4):
            pick[4 * q + i, q, i // 2, i % 2] = 1
    return pick.reshape(8, 4 * P)


def reach(k):
    outs = [o for o in range(HG) if 0 <= R * o + k - PAD < H]
    return outs[0], len(outs), R * outs[0] + k - PAD


ALL_TAPS = sorted(((kh, kw) for kh in range(KS) for kw in range(KS)),
                  key=lambda t: -reach(t[0])[1] * reach(t[1])[1])
PE_TAPS = [(3, 3)] + [t for t in ALL_TAPS[3:] if t != (3, 3)][-23:]
CENTER_AT = 8
DVE_TAPS = [t for t in ALL_TAPS if t not in PE_TAPS]


MIX_ORDER = [(0, 0, 0), (0, 0, 1), (4, 1, 0), (4, 1, 1), (1, 0, 0), (0, 1, 0), (1, 0, 1), (0, 1, 1),
             (2, 0, 0), (2, 0, 1), (1, 1, 0), (3, 0, 0), (3, 0, 1), (1, 1, 1), (2, 1, 0), (2, 1, 1),
             (3, 1, 0), (3, 1, 1)]


def build(nc, x_tok, x_par, x_chan, early, late, rows, const, pick, out):
    with ExitStack() as ctx:
        def sb(name, shape, dt=F32):
            return ctx.enter_context(nc.sbuf_tensor(name, shape, dt))

        def sem(name):
            return ctx.enter_context(nc.semaphore(name))

        xt = sb("xt", [P, TILES, C])
        xp = sb("xp", [P, TILES, C])
        xc = sb("xc", [C, TILES, P])
        ew = sb("ew", [P, EARLY_N])
        lw = sb("lw", [P, LATE_N + P])
        rb = sb("rb", [P, len(ROWS), C])
        cs = sb("cs", [P, CONST_N])
        ones = sb("ones", [P, P])
        pk = sb("pk", [8, 4 * P])
        negpick = sb("negpick", [8, 4 * P], F32R)
        mhalf = sb("mhalf", [P, TILES])
        spare0 = sb("spare0", [P, 1])
        spare = sb("spare", [P, 4])
        stats = sb("stats", [P, TILES, 6])
        mv = sb("mv", [P, TILES, 2])
        vareps = sb("vareps", [P, TILES])
        rstd = sb("rstd", [P, TILES])
        xn = sb("xn", [P, TILES, C])
        xg = sb("xg", [P, TILES, C])
        xl = sb("xl", [P, TILES, C])
        qbias = sb("qbias", [C, P])
        q_img = sb("q_img", [C, H, 2, W // 2, B])
        diag = sb("diag", [C, len(PE_TAPS), P])
        acc = sb("acc", [C, 2, HG, HG * B])
        accs = sb("accs", [C, KEYS * B])
        conv = sb("conv", [C, KEYS, B])
        og = sb("og", [C, B, KEYS])
        pwb = sb("pwb", [C, 2, P])
        th = sb("th", [P, 2, B, KEYS])
        dist = sb("dist", [P, 2, B, KEYS])
        absd = sb("absd", [P, 3, B, KEYS])
        hat = sb("hat", [P, 3, B, KEYS])
        wt = sb("wt", [P, 2, B, KEYS])
        it = sb("it", [C, B, 2, KEYS])
        gmlp = sb("gmlp", [C, C])
        fw = sb("fw", [C, 4, C])
        fb = sb("fb", [C, 3])
        bd1 = sb("bd1", [C, 2, 8, 16])
        ab = sb("ab", [C, 4, 16])
        abd = sb("abd", [C, 4, 8, 16])
        m1 = sb("m1", [C, C])
        fl = sb("fl", [C, 4, C])
        nw1 = sb("nw1", [C, C])
        vrow = sb("vrow", [P, C])
        vrowm = sb("vrowm", [P, C])
        vm = sb("vm", [P, B, C])
        mlp_row = sb("mlp_row", [P, C])
        qh = sb("qh", [C, B, 2, P])
        qhr = sb("qhr", [C, B, 2, P], F32R)
        kbd = sb("kbd", [C, B, 4, KEYS])
        kbr = sb("kbr", [C, B, 4, KEYS], F32R)
        vbd = sb("vbd", [P, B, C])
        mx = sb("mx", [P, 2, 2, 2, 4])
        pt = sb("pt", [P, 2, 4, 2 * P])
        rs = sb("rs", [C, 2, 2 * P])
        at = sb("at", [C, 2, 2, P])
        mxt = sb("mxt", [8, 2, 2, P], F32R)
        z = sb("z", [P, TILES, C])
        stats2 = sb("stats2", [P, TILES, 6])
        mv2 = sb("mv2", [P, TILES, 2])
        vareps2 = sb("vareps2", [P, TILES])
        rstd2 = sb("rstd2", [P, TILES])
        u = sb("u", [P, TILES, C])
        ug = sb("ug", [P, TILES, C])
        x1 = sb("x1", [P, TILES, C])
        ct = sb("ct", [C, 2, 2, 2, P])
        o1k = sb("o1k", [C, 2, 2, 2, P])
        o1n = sb("o1n", [C, 2, 2, 2, P])
        yc = sb("yc", [C, 2, 2, 2, P])
        ys = sb("ys", [C, 2, 2, 2, P])
        yd = sb("yd", [P, 2, 2, 2, C])
        lim = sb("lim", [C, 2])
        fin = sb("fin", [P, TILES, C])

        bank = [ctx.enter_context(nc.psum_tensor(f"bank{i}", [P, 512], F32)) for i in range(8)]
        ps_s = bank[0:2]
        ps_t = bank[2:4]
        ps_av = bank[4]
        ps_out = bank[5]
        ps_mix = bank[6:8]

        av_bank = (ps_av, ps_mix[0])
        out_bank = (ps_out, ps_out, ps_s[0], ps_s[1])
        mix_bank = ((ps_mix[1], ps_t[0]), (ps_t[1], ps_av))

        def const_ap(name):
            return cs[:, CONST[name][0]:CONST[name][1]]

        def late_ap(name):
            return lw[:, LATE[name][0]:LATE[name][1]]

        def vec(name):
            i = P + NTAP + VEC[name]
            return ew[:, i:i + 1]

        wq = ew[:, 0:P]
        ident, cas = const_ap("ident"), const_ap("cas")
        wsd = const_ap("wsd").rearrange("p (a n) -> p a n", a=2)
        winv = const_ap("winv").rearrange("p (a n) -> p a n", a=2)
        dconst = const_ap("dist").rearrange("p (a n) -> p a n", a=2)
        kmask = const_ap("kmask")
        block8, half8 = const_ap("block"), const_ap("half")
        mo_g = lw[:, LATE["mo"][0]:LATE["mo"][0] + 2 * P]
        wqq, wvk, wvv, wmlp = (fw[:, i, :] for i in range(4))
        w0, w1, wk, wn = (fl[:, i, :] for i in range(4))

        d_x, d_early, d_rows, d_ident, d_const, d_late, d_xp, d_xc, d_pick, d_out = (
            sem("d_" + n) for n in ("x0", "early", "rows", "ident", "const", "late", "xp", "xc", "pick", "out"))
        d_x = [d_x] + [sem(f"d_x{b}") for b in range(1, B)]
        s_ones, s_mhalf, s_spare = sem("s_ones"), sem("s_mhalf"), sem("s_spare")
        s_stats, s_mv, s_var, s_rstd = sem("s_stats"), sem("s_mv"), sem("s_var"), sem("s_rstd")
        s_xn, s_xg, s_xl = sem("s_xn"), sem("s_xg"), sem("s_xl")
        s_colsum, s_qbias, s_qps, s_qimg = sem("s_colsum"), sem("s_qbias"), sem("s_qps"), sem("s_qimg")
        s_diag, s_acc, s_accs = sem("s_diag"), [sem("s_acc0"), sem("s_acc1")], sem("s_accs")
        s_convps, s_conv, s_og = sem("s_convps"), sem("s_conv"), sem("s_og")
        s_pwb, s_gmlp, s_bd1, s_ab, s_abd = (sem("s_" + n) for n in ("pwb", "gmlp", "bd1", "ab", "abd"))
        s_fwps, s_fw, s_fbps, s_fb, s_m1 = (sem("s_" + n) for n in ("fwps", "fw", "fbps", "fb", "m1"))
        s_gps, s_g, s_rows, s_flps, s_fl = (sem("s_" + n) for n in ("gps", "g", "rows", "flps", "fl"))
        s_xp, s_xc, s_lim, s_vm, s_negid = (sem("s_" + n) for n in ("xp", "xc", "lim", "vm", "negid"))
        s_qhps, s_qh, s_qhr = sem("s_qhps"), sem("s_qh"), sem("s_qhr")
        s_off, s_th, s_dist, s_abs, s_hat, s_wt = (
            sem("s_" + n) for n in ("off", "th", "dist", "abs", "hat", "wt"))
        s_itps, s_it, s_kps, s_kbd, s_kbr, s_vps, s_vbd = (
            sem("s_" + n) for n in ("itps", "it", "kps", "kbd", "kbr", "vps", "vbd"))
        s_mxtps, s_mxt = sem("s_mxtps"), sem("s_mxt")
        s_s, s_mx, s_st, s_exp, s_av, s_rs, s_at = (
            sem("s_" + n) for n in ("s", "mx", "st", "exp", "av", "rs", "at"))
        s_out, s_z, s_stats2, s_mv2, s_var2, s_rstd2, s_u, s_ug, s_x1 = (
            sem("s_" + n) for n in ("out", "z", "stats2", "mv2", "var2", "rstd2", "u", "ug", "x1"))
        s_ctps, s_ct, s_tps, s_o1k, s_o1n, s_yps, s_yc, s_ys, s_ydps, s_yd, s_fps, s_fin = (
            [sem(f"s_{n}{par}") for par in range(2)]
            for n in ("ctps", "ct", "tps", "o1k", "o1n", "yps", "yc", "ys", "ydps", "yd", "fps", "fin"))

        def window(kh, kw):
            oh, nh, ih = reach(kh)
            ow, nw, iw = reach(kw)
            src = q_img[:, ih:ih + R * nh - 1:R, iw % 2, iw // 2:iw // 2 + nw, :].rearrange("c h w b -> c h (w b)")
            return src, slice(oh, oh + nh), slice(B * ow, B * (ow + nw))

        def tap(kh, kw):
            i = P + kh * KS + kw
            return ew[:, i:i + 1]

        block = ctx.enter_context(nc.Block())

        @block.sync
        def _(sp):
            for b in range(B):
                sp.dma_start(xt[:, 2 * b:2 * b + 2, :], x_tok[:, 2 * b:2 * b + 2, :]).then_inc(d_x[b], 16)
            sp.dma_start(rb[:].rearrange("p a n -> p (a n)"), rows.broadcast_to([P, len(ROWS) * C])).then_inc(d_rows, 16)
            sp.dma_start(lw[:, 0:LATE_N], late).then_inc(d_late, 16)
            sp.dma_start(cs[:, P:CONST_N], const[:, P:CONST_N]).then_inc(d_const, 16)
            sp.dma_start(pk[:], pick).then_inc(d_pick, 16)
            sp.dma_start(xc[:], x_chan).then_inc(d_xc, 16)
            sp.dma_start(xp[:], x_par).then_inc(d_xp, 16)
            for g in range(2):
                for par in range(2):
                    sp.wait_ge(s_fin[par], g + 1)
                    sp.dma_start(out[:, 4 * g + par:4 * g + par + 3:2, :],
                                 fin[:, 4 * g + par:4 * g + par + 3:2, :]).then_inc(d_out, 16)
            sp.wait_ge(d_out, 64)

        @block.gpsimd
        def _(pool):
            pool.memset(ones[:], 1.0).then_inc(s_ones, 1)
            pool.memset(spare0[:], 0.0).then_inc(s_spare, 1)
            pool.memset(mhalf[:], -0.5).then_inc(s_mhalf, 1)
            pool.wait_ge(s_mhalf, 1)
            for g in range(2):
                pool.wait_ge(s_var, g + 1)
                pool.tensor_tensor(rstd[:, 4 * g:4 * g + 4], vareps[:, 4 * g:4 * g + 4],
                                   mhalf[:, 4 * g:4 * g + 4], ALU.pow).then_inc(s_rstd, 1)
            pool.wait_ge(d_rows, 16)
            for g in range(2):
                pool.wait_ge(s_xn, 4 * g + 4)
                t = slice(4 * g, 4 * g + 4)
                pool.tensor_tensor(xg[:, t, :], xn[:, t, :], rb[:, 0:1, :].broadcast_to([P, 4, C]),
                                   ALU.mult).then_inc(s_xg, 1)
                pool.wait_ge(s_xg, g + 1)
                pool.tensor_tensor(xl[:, t, :], xg[:, t, :], rb[:, 1:2, :].broadcast_to([P, 4, C]),
                                   ALU.add).then_inc(s_xl, 1)
            pool.wait_ge(d_late, 16)
            pool.wait_ge(d_early, 16)
            pool.tensor_tensor(gmlp[:], late_ap("mlp"), vec("ln_g").broadcast_to([C, C]), ALU.mult).then_inc(s_gmlp, 1)
            for k in range(2):
                pool.tensor_copy(pwb[:, k, :], vec(f"pw{k}").broadcast_to([C, P])).then_inc(s_pwb, 1)
            for i, name in enumerate(("w2", "w2T")):
                a = lw[:, LATE[name][0]:LATE[name][0] + 16]
                b = lw[:, LATE[name][0] + 16:LATE[name][1]]
                pool.tensor_tensor(ab[:, 2 * i, :], a, b, ALU.add).then_inc(s_ab, 1)
                pool.tensor_tensor(ab[:, 2 * i + 1, :], a, b, ALU.subtract).then_inc(s_ab, 1)
            pool.wait_ge(d_const, 16)
            for i in range(2):
                w = lw[:, LATE["w1"][0] + 16 * i:LATE["w1"][0] + 16 * i + 16]
                pool.tensor_tensor(bd1[:, i], w.unsqueeze(1).broadcast_to([C, 8, 16]),
                                   block8.unsqueeze(2).broadcast_to([C, 8, 16]), ALU.mult).then_inc(s_bd1, 1)
            pool.wait_ge(s_ab, 4)
            for i in range(4):
                pool.tensor_tensor(abd[:, i], ab[:, i, :].unsqueeze(1).broadcast_to([C, 8, 16]),
                                   half8.unsqueeze(2).broadcast_to([C, 8, 16]), ALU.mult).then_inc(s_abd, 1)
            pool.wait_ge(s_abd, 4)
            pool.wait_ge(d_ident, 16)
            pool.tensor_tensor(m1[:], ident, abd[:, 1].rearrange("p a n -> p (a n)"), ALU.add).then_inc(s_m1, 1)
            pool.wait_ge(d_xp, 16)
            pool.wait_ge(d_xc, 16)
            for g in range(2):
                t = slice(4 * g, 4 * g + 4)
                pool.tensor_tensor(xc[:, t, :], xc[:, t, :], vec("mo_b").unsqueeze(1).broadcast_to([C, 4, P]),
                                   ALU.add).then_inc(s_xc, 1)
                pool.tensor_tensor(xp[:, t, :], xp[:, t, :], rb[:, 3:4, :].broadcast_to([P, 4, C]),
                                   ALU.add).then_inc(s_xp, 1)
            for b in range(B):
                pool.wait_ge(s_var2, b + 1)
                pool.tensor_tensor(rstd2[:, 2 * b:2 * b + 2], vareps2[:, 2 * b:2 * b + 2],
                                   mhalf[:, 0:2], ALU.pow).then_inc(s_rstd2, 1)

        @block.scalar
        def _(act):
            act.dma_start(ew[:], early).then_inc(d_early, 16)
            act.dma_start(cs[:, 0:P], const[:, 0:P]).then_inc(d_ident, 16)
            act.wait_ge(s_spare, 1)
            act.activation(spare[:, 2:3], spare0[:, 0:1], ACT.Copy)
            act.wait_ge(d_early, 16)
            act.wait_ge(d_ident, 16)
            for n, (kh, kw) in enumerate(PE_TAPS):
                act.activation(diag[:, n, :], ident, ACT.Copy, scale=tap(kh, kw)).then_inc(s_diag, 1)
            act.wait_ge(d_pick, 16)
            act.mul(negpick[:], pk[:], -1.0).then_inc(s_negid, 1)
            act.wait_ge(s_fwps, 1)
            act.copy(fw[:], ps_mix[0][:].rearrange("p (a n) -> p a n", a=4)).then_inc(s_fw, 1)

            def queries(g):
                act.wait_ge(s_qhps, g + 1)
                src = (ps_av, ps_out)[g][:].rearrange("p (b a n) -> p b a n", b=2, a=2)
                act.activation(qh[:, 2 * g:2 * g + 2], src, ACT.Identity, bias=fb[:, 0:1]).then_inc(s_qh, 1)
                act.activation(qhr[:, 2 * g:2 * g + 2], src, ACT.Identity, bias=fb[:, 0:1]).then_inc(s_qhr, 1)

            act.activation(spare[:, 0:1], spare0[:, 0:1], ACT.Gelu)
            act.wait_ge(s_conv, 1)
            act.activation(og[:], conv[:].rearrange("c n b -> c b n"), ACT.Gelu, bias=vec("dw_b")).then_inc(s_og, 1)
            act.wait_ge(s_fb, 1)
            queries(0)
            for n, k in enumerate((1, 0)):
                act.wait_ge(s_off, 2)
                act.activation(th[:, k], ps_t[0][:, 256 * k:256 * k + 256].rearrange("p (b n) -> p b n", b=B),
                               ACT.Tanh).then_inc(s_th, 1)
            for i in range(3):
                act.wait_ge(s_dist, min(i, 1) + 1)
                act.activation(absd[:, i], dist[:, min(i, 1)], ACT.Abs,
                               bias=const_ap("lower") if i == 2 else 0.0).then_inc(s_abs, 1)
            queries(1)
            act.wait_ge(s_flps, 1)
            act.copy(fl[:], ps_mix[1][:].rearrange("p (a n) -> p a n", a=4)).then_inc(s_fl, 1)
            act.mul(nw1[:], ps_mix[1][:, P:2 * P], -1.0).then_inc(s_fl, 1)
            act.activation(spare[:, 1:2], spare0[:, 0:1], ACT.Exp)
            for b in range(B):
                act.wait_ge(s_kbd, b + 1)
                act.copy(kbr[:, b], kbd[:, b]).then_inc(s_kbr, 1)
            act.wait_ge(s_gps, 1)
            act.copy(lw[:, LATE_N:LATE_N + P], ps_out[:, 0:P]).then_inc(s_g, 1)

            def exp(b):
                if b >= 2:
                    act.wait_ge(s_av, b - 1)
                for a in range(2):
                    act.wait_ge(s_st, 2 * b + a + 1)
                    act.activation(pt[:, b % 2, 2 * a:2 * a + 2, :],
                                   ps_t[a][:].rearrange("p (i n) -> p i n", i=2), ACT.Exp).then_inc(s_exp, 1)

            def gelu(b):
                act.wait_ge(s_u, 2 * b + 2)
                t = slice(2 * b, 2 * b + 2)
                act.activation(ug[:, t, :], u[:, t, :], ACT.Gelu).then_inc(s_ug, 1)

            def sums(g, par):
                act.wait_ge(s_ctps[par], g + 1)
                act.copy(ct[:, g, par], mix_bank[g][par][:, 0:256].rearrange("p (b n) -> p b n", b=2)
                         ).then_inc(s_ct[par], 1)

            def relu_k(g, par):
                act.wait_ge(s_tps[par], g + 1)
                act.activation(o1k[:, g, par], mix_bank[g][par][:, 256:512].rearrange("p (b n) -> p b n", b=2),
                               ACT.Relu, bias=vec("b1k")).then_inc(s_o1k[par], 1)

            def back(g, par):
                act.wait_ge(s_ydps[par], g + 1)
                act.copy(yd[:, g, par], mix_bank[g][par][:, 256:512].rearrange("p (b n) -> p b n", b=2)
                         ).then_inc(s_yd[par], 1)

            exp(0)
            exp(1)
            exp(2)
            exp(3)
            gelu(0)
            gelu(1)
            sums(0, 0)
            sums(0, 1)
            gelu(2)
            gelu(3)
            relu_k(0, 0)
            relu_k(0, 1)
            sums(1, 0)
            sums(1, 1)
            relu_k(1, 0)
            relu_k(1, 1)
            back(0, 0)
            back(0, 1)
            back(1, 0)
            back(1, 1)

        @block.vector
        def _(dve):
            for g in range(2):
                for i in range(4 * g, 4 * g + 4):
                    if i % 2 == 0:
                        dve.wait_ge(d_x[i // 2], 16)
                    dve.bn_stats(stats[:, i, :], xt[:, i, :]).then_inc(s_stats, 1)
                for i in range(4 * g, 4 * g + 4):
                    dve.wait_ge(s_stats, i + 1)
                    dve.bn_aggr(mv[:, i, :], stats[:, i, :]).then_inc(s_mv, 1)
                dve.wait_ge(s_mv, 4 * g + 4)
                dve.tensor_scalar(vareps[:, 4 * g:4 * g + 4], mv[:, 4 * g:4 * g + 4, 1], EPS, None,
                                  ALU.add).then_inc(s_var, 1)

            def normalise(g):
                dve.wait_ge(s_rstd, g + 1)
                for i in range(4 * g, 4 * g + 4):
                    dve.tensor_scalar(xn[:, i, :], xt[:, i, :], mv[:, i, 0:1], rstd[:, i:i + 1],
                                      ALU.subtract, ALU.mult).then_inc(s_xn, 1)

            normalise(0)
            dve.wait_ge(s_colsum, 1)
            dve.wait_ge(d_rows, 16)
            dve.wait_ge(d_early, 16)
            dve.scalar_tensor_tensor(out=qbias[:], in0=ps_t[0][:, 0:P], scalar=vec("ln_b"),
                                     in1=rb[:, 2, :], op0=ALU.mult, op1=ALU.add).then_inc(s_qbias, 1)
            normalise(1)
            dve.wait_ge(s_qbias, 1)
            for g in range(2):
                dve.wait_ge(s_qps, g + 1)
                for a in range(2):
                    dve.scalar_tensor_tensor(
                        out=q_img[:, 8 * a:8 * a + 8, :, :, 2 * g:2 * g + 2].rearrange("c h p w b -> c b (h p w)"),
                        in0=ps_s[g][:].rearrange("c (b a n) -> c a b n", b=2, a=2)[:, a], scalar=vec("ln_g"),
                        in1=qbias[:].unsqueeze(1).broadcast_to([C, 2, P]),
                        op0=ALU.mult, op1=ALU.add).then_inc(s_qimg, 1)
            dve.wait_ge(s_qimg, 4)
            for n, (kh, kw) in enumerate(DVE_TAPS):
                src, oh, ow = window(kh, kw)
                a = n % 2
                if n < 2:
                    dve.tensor_scalar(acc[:, a], src, tap(kh, kw), None, ALU.mult).then_inc(s_acc[a], 1)
                    continue
                dst = acc[:, a, oh, ow]
                dve.wait_ge(s_acc[a], n // 2)
                dve.scalar_tensor_tensor(out=dst, in0=src, scalar=tap(kh, kw), in1=dst, op0=ALU.mult,
                                         op1=ALU.add).then_inc(s_acc[a], 1)
            dve.wait_ge(s_acc[0], (len(DVE_TAPS) + 1) // 2)
            dve.wait_ge(s_acc[1], len(DVE_TAPS) // 2)
            dve.tensor_tensor(accs[:], acc[:, 0].rearrange("c h w -> c (h w)"),
                              acc[:, 1].rearrange("c h w -> c (h w)"), ALU.add).then_inc(s_accs, 1)
            dve.wait_ge(s_accs, 1)
            dve.wait_ge(s_convps, 1)
            dve.tensor_tensor(conv[:].rearrange("c n b -> c (n b)"), ps_t[1][:, 0:256], accs[:], ALU.add).then_inc(s_conv, 1)
            dve.wait_ge(s_fbps, 1)
            i = P + NTAP + VEC["mq_b"]
            dve.tensor_tensor(fb[:], ps_mix[1][:, 0:3], ew[:, i:i + 3], ALU.add).then_inc(s_fb, 1)
            dve.wait_ge(s_fb, 1)
            dve.tensor_scalar(lim[:, 0:1], fb[:, 2:3], -1.0, -SPARSITY, ALU.mult, ALU.add).then_inc(s_lim, 1)
            dve.tensor_scalar(lim[:, 1:2], fb[:, 2:3], -1.0, SPARSITY, ALU.mult, ALU.add).then_inc(s_lim, 1)
            for i, k in enumerate((1, 0)):
                dve.wait_ge(s_th, i + 1)
                dve.scalar_tensor_tensor(out=dist[:, i], in0=th[:, k], scalar=COORD,
                                         in1=dconst[:, i:i + 1, :].broadcast_to([P, B, KEYS]),
                                         op0=ALU.mult, op1=ALU.add).then_inc(s_dist, 1)
            for i in range(3):
                dve.wait_ge(s_abs, i + 1)
                dve.tensor_scalar(hat[:, i], absd[:, i], -1.0, 0.0, ALU.add, ALU.min).then_inc(s_hat, 1)
            for i in range(2):
                dve.wait_ge(s_hat, i + 2)
                dve.tensor_tensor(wt[:, i], hat[:, 0], hat[:, 1 + i], ALU.mult).then_inc(s_wt, 1)
            dve.wait_ge(s_itps, 1)
            dve.tensor_copy(it[:, :, 0, :], ps_mix[0][:, 0:256].rearrange("p (b n) -> p b n", b=B)).then_inc(s_it, 1)
            dve.wait_ge(s_it, 1)
            dve.tensor_copy(it[:, :, 1, :], it[:, :, 0, :]).then_inc(s_it, 1)
            def row_max(b):
                if b >= 2:
                    dve.wait_ge(s_mxtps, 2 * b - 2)
                for a in range(2):
                    dve.wait_ge(s_s, 2 * b + a + 1)
                    dve.tensor_reduce(mx[:, b % 2, a], ps_s[a][:].rearrange("p (q i n) -> p q i n", q=2, n=KEYS),
                                      AX_X, ALU.max).then_inc(s_mx, 1)

            def turned_max(b):
                if b >= 2:
                    dve.wait_ge(s_st, 2 * b - 2)
                for a in range(2):
                    dve.wait_ge(s_mxtps, 2 * b + a + 1)
                    dve.tensor_copy(mxt[:, b % 2, a], ps_s[a][0:8, 0:P]).then_inc(s_mxt, 1)

            def divide(b):
                dve.wait_ge(s_av, b + 1)
                if b >= 2:
                    dve.wait_ge(s_at, b - 1)
                    dve.wait_ge(s_out, b - 1)
                dve.reciprocal(rs[:, b % 2], av_bank[b % 2][:, 256:512]).then_inc(s_rs, 1)
                dve.wait_ge(s_rs, b + 1)
                dve.tensor_tensor(at[:, b % 2].rearrange("c a n -> c (a n)"), av_bank[b % 2][:, 0:256],
                                  rs[:, b % 2], ALU.mult).then_inc(s_at, 1)

            def keys(b):
                dve.scalar_tensor_tensor(out=kbd[:, b], in0=ps_av[:, KEYS * b:KEYS * b + KEYS].unsqueeze(1)
                                         .broadcast_to([C, 4, KEYS]), scalar=fb[:, 1:2],
                                         in1=kmask.unsqueeze(2).broadcast_to([C, 4, KEYS]), op0=ALU.add,
                                         op1=ALU.mult).then_inc(s_kbd, 1)

            dve.wait_ge(s_kps, 1)
            for b in range(B):
                keys(b)
            row_max(0)
            turned_max(0)
            dve.wait_ge(s_gps, 1)
            dve.wait_ge(s_g, 1)
            dve.tensor_tensor(mlp_row[:], ps_out[:, P:2 * P], rb[:, 4, :], ALU.add).then_inc(s_rows, 1)
            dve.tensor_tensor(vrow[:], ps_out[:, 2 * P:3 * P], rb[:, 5, :], ALU.add).then_inc(s_rows, 1)
            dve.wait_ge(s_rows, 2)
            dve.tensor_tensor(vrowm[:], vrow[:], const_ap("vmask"), ALU.mult).then_inc(s_rows, 1)
            dve.wait_ge(s_vps, 1)
            dve.tensor_tensor(vm[:], ps_mix[1][:].rearrange("p (b n) -> p b n", b=B),
                              const_ap("vmask").unsqueeze(1).broadcast_to([P, B, C]), ALU.mult).then_inc(s_vm, 1)
            dve.wait_ge(s_vm, 1)
            dve.wait_ge(s_rows, 3)
            dve.tensor_tensor(vbd[:], vm[:], vrowm[:].unsqueeze(1).broadcast_to([P, B, C]), ALU.add).then_inc(s_vbd, 1)

            def residual(b):
                t = slice(2 * b, 2 * b + 2)
                dve.wait_ge(s_out, b + 1)
                dve.wait_ge(s_xp, b // 2 + 1)
                dve.tensor_tensor(z[:, t, :], out_bank[b][:].rearrange("p (i n) -> p i n", i=2)[:, :, 0:C],
                                  xp[:, t, :], ALU.add).then_inc(s_z, 1)
                dve.wait_ge(s_z, b + 1)
                for i in (2 * b, 2 * b + 1):
                    dve.bn_stats(stats2[:, i, :], z[:, i, :]).then_inc(s_stats2, 1)
                for i in (2 * b, 2 * b + 1):
                    dve.wait_ge(s_stats2, i + 1)
                    dve.bn_aggr(mv2[:, i, :], stats2[:, i, :]).then_inc(s_mv2, 1)
                dve.wait_ge(s_mv2, 2 * b + 2)
                dve.tensor_scalar(vareps2[:, t], mv2[:, t, 1], EPS, None, ALU.add).then_inc(s_var2, 1)

            def mlp_in(b):
                dve.wait_ge(s_rstd2, b + 1)
                for i in range(2):
                    dve.scalar_tensor_tensor(out=u[:, 2 * b + i, :], in0=out_bank[b][:, 256 * i + C:256 * i + 2 * C],
                                             scalar=rstd2[:, 2 * b + i:2 * b + i + 1], in1=mlp_row[:],
                                             op0=ALU.mult, op1=ALU.add).then_inc(s_u, 1)

            def block_out(b):
                t = slice(2 * b, 2 * b + 2)
                dve.wait_ge(s_ug, b + 1)
                dve.tensor_tensor(x1[:, t, :], ug[:, t, :], z[:, t, :], ALU.add).then_inc(s_x1, 1)

            def relu_n(g, par):
                dve.wait_ge(s_tps[par], g + 1)
                dve.wait_ge(s_o1k[par], g + 1)
                dve.tensor_scalar(o1n[:, g, par], mix_bank[g][par][:, 256:512].rearrange("p (b n) -> p b n", b=2),
                                  vec("b1n"), 0.0, ALU.add, ALU.max).then_inc(s_o1n[par], 1)

            def threshold(g, par):
                y = mix_bank[g][par][:, 0:256].rearrange("p (b n) -> p b n", b=2)
                dve.wait_ge(s_yps[par], g + 1)
                dve.tensor_scalar(yc[:, g, par], y, lim[:, 0:1], lim[:, 1:2], ALU.max, ALU.min
                                  ).then_inc(s_yc[par], 1)
                dve.wait_ge(s_yc[par], g + 1)
                dve.tensor_tensor(ys[:, g, par], y, yc[:, g, par], ALU.subtract).then_inc(s_ys[par], 1)

            def finish(g, par):
                dve.wait_ge(s_fps[par], g + 1)
                t = slice(4 * g + par, 4 * g + par + 3, 2)
                dve.tensor_tensor(fin[:, t, :], mix_bank[g][par][:, 0:256].rearrange("p (b n) -> p b n", b=2),
                                  x1[:, t, :], ALU.add).then_inc(s_fin[par], 1)

            dve.wait_ge(s_lim, 2)
            row_max(1)
            turned_max(1)
            row_max(2)
            divide(0)
            turned_max(2)
            row_max(3)
            divide(1)
            turned_max(3)
            residual(0)
            mlp_in(0)
            divide(2)
            residual(1)
            mlp_in(1)
            block_out(0)
            divide(3)
            block_out(1)
            residual(2)
            mlp_in(2)
            residual(3)
            mlp_in(3)
            block_out(2)
            relu_n(0, 0)
            block_out(3)
            relu_n(0, 1)
            threshold(0, 0)
            relu_n(1, 0)
            threshold(0, 1)
            relu_n(1, 1)
            threshold(1, 0)
            finish(0, 0)
            finish(0, 1)
            threshold(1, 1)
            finish(1, 0)
            finish(1, 1)

        @block.tensor
        def _(pe):
            def mm(o, lhsT, rhs, start=True, stop=True):
                return pe.matmul(o, lhsT, rhs, start=start, stop=stop, skip_group_check=True)

            def warm(bank_, n):
                for _ in range(n):
                    mm(bank_[:, 0:P], ones[:], ones[:])

            pe.wait_ge(s_ones, 1)
            warm(ps_out, 6)
            pe.wait_ge(d_early, 16)
            mm(ps_t[0][:, 0:P], ones[:], wq).then_inc(s_colsum, 1)
            warm(ps_out, 6)
            for g in range(2):
                for i in range(4):
                    pe.wait_ge(s_xn, 4 * g + i + 1)
                    last = mm(ps_s[g][:, P * i:P * i + P], xn[:, 4 * g + i, :], wq, start=(i == 0))
                last.then_inc(s_qps, 1)
            pe.wait_ge(d_late, 16)
            pe.wait_ge(d_const, 16)
            mm(ps_mix[0][:, 0:P], late_ap("wqT"), late_ap("mq"))
            mm(ps_mix[0][:, P:2 * P], late_ap("wvT"), late_ap("mk"), start=False)
            mm(ps_mix[0][:, 2 * P:3 * P], late_ap("wvT"), late_ap("mv"), start=False)
            pe.wait_ge(s_qimg, 4)
            cps = ps_t[1][:, 0:256].rearrange("c (h w) -> c h w", h=HG)
            for n, (kh, kw) in enumerate(PE_TAPS):
                src, oh, ow = window(kh, kw)
                if n == CENTER_AT:
                    pe.wait_ge(s_gmlp, 1)
                    mm(ps_mix[0][:, 3 * P:4 * P], const_ap("center"), gmlp[:], start=False).then_inc(s_fwps, 1)
                pe.wait_ge(s_diag, n + 1)
                last = mm(cps[:, oh, ow], diag[:, n, :], src, start=(n == 0), stop=(n == len(PE_TAPS) - 1))
            last.then_inc(s_convps, 1)
            pe.wait_ge(s_m1, 1)
            mm(ps_mix[1][:, 0:1], late_ap("mq"), vec("bq"))
            mm(ps_mix[1][:, 1:2], late_ap("mk"), vec("bv"), start=False)
            mm(ps_mix[1][:, 2:3], m1[:], vec("b2k"), start=False).then_inc(s_fbps, 1)
            pe.wait_ge(s_fw, 1)
            for g in range(2):
                pe.wait_ge(s_xl, g + 1)
                for i in range(4):
                    o = (ps_av, ps_out)[g][:, 256 * (i // 2):256 * (i // 2) + 256]
                    last = mm(o.rearrange("p (a m) -> p a m", a=2)[:, :, 64 * (i % 2):64 * (i % 2) + 64], wqq,
                              xl[:, 4 * g + i, :].rearrange("p (h a w) -> p a h w", a=2, w=8), start=(i == 0))
                last.then_inc(s_qhps, 1)
            pe.wait_ge(s_pwb, 2)
            pe.wait_ge(s_qbias, 1)
            pe.wait_ge(s_og, 1)
            for k in (1, 0):
                mm(ps_t[0][:, 256 * k:256 * k + 256], pwb[:, k, :], og[:].rearrange("c b n -> c (b n)"),
                   start=(k == 1)).then_inc(s_off, 1)
            pe.wait_ge(s_bd1, 2)
            pe.wait_ge(s_abd, 4)
            pe.wait_ge(s_fb, 1)
            for i in range(2):
                mm(ps_mix[1][:, P * i:P * i + P], cas, bd1[:, i].rearrange("p a n -> p (a n)"), start=(i == 0))
            at_, bt_ = (abd[:, i].rearrange("p a n -> p (a n)") for i in (2, 3))
            mm(ps_mix[1][:, 2 * P:3 * P], at_, m1[:], start=False)
            mm(ps_mix[1][:, 3 * P:4 * P], bt_, m1[:], start=False, stop=False)
            mm(ps_mix[1][:, 3 * P:4 * P], at_, ident, start=False).then_inc(s_flps, 1)
            warm(ps_s[0], 5)
            pe.wait_ge(s_wt, 2)
            for b in range(B):
                for i in range(2):
                    for c in range(2):
                        last = pe.matmul(ps_mix[0][KEYS * c:KEYS * c + KEYS, KEYS * b:KEYS * b + KEYS],
                                         wt[:, i, b, :], xt[:, 2 * b + i, c:C:2], start=(b == 0 and i == 0),
                                         stop=(i == 1), skip_group_check=True, tile_position=(0, KEYS * c))
            last.then_inc(s_itps, 1)
            pe.wait_ge(s_qhr, 2)
            mm(ps_out[:, 0:P], late_ap("moT"), wmlp)
            mm(ps_out[:, P:2 * P], vec("ln_b").broadcast_to([C, P]), late_ap("mlp"), start=False)
            mm(ps_out[:, 2 * P:3 * P], vec("bv").broadcast_to([C, P]), late_ap("mv"), start=False).then_inc(s_gps, 1)
            pe.wait_ge(s_it, 1)
            mm(ps_av[:, 0:256], wvk, it[:, :, 0, :]).then_inc(s_kps, 1)
            pe.wait_ge(s_it, 2)
            pe.wait_ge(s_fl, 2)
            for b in range(B):
                last = mm(ps_mix[1][:, P * b:P * b + P], it[:, b].rearrange("c i n -> c (i n)"), wvv,
                          start=(b == 0))
            last.then_inc(s_vps, 1)
            warm(ps_s[0], 1)

            def scores_q(b):
                pe.wait_ge(s_kbr, b + 1)
                pe.wait_ge(s_qhr, b // 2 + 1)
                if b >= 1:
                    pe.wait_ge(s_mxt, 2 * b)
                for a in range(2):
                    r = slice(64 * a, 64 * a + 64)
                    for q in range(2):
                        last = mm(ps_s[a][:, 256 * q:256 * q + 256], qhr[r, b, q, :],
                                  kbr[r, b].rearrange("c i n -> c (i n)"), start=(q == 0))
                    last.then_inc(s_s, 1)

            def scores_k(b, a):
                if b >= 1:
                    pe.wait_ge(s_exp, 2 * b - 1 + a)
                r = slice(64 * a, 64 * a + 64)
                for i in range(2):
                    mm(ps_t[a][:, 256 * i:256 * i + 256],
                       kbd[r, b, 2 * i:2 * i + 2].rearrange("c i n -> c (i n)"),
                       qh[r, b].rearrange("c a n -> c (a n)"), start=(i == 0), stop=False)

            def turn_max(b):
                for a in range(2):
                    pe.wait_ge(s_mx, 2 * b + a + 1)
                    pe.transpose(ps_s[a][0:8, 0:P], mx[:, b % 2, a].rearrange("p q i -> p (q i)"),
                                 ident).then_inc(s_mxtps, 1)

            def shift(b):
                if b == 0:
                    pe.wait_ge(s_negid, 1)
                for a in range(2):
                    pe.wait_ge(s_mxt, 2 * b + a + 1)
                    for i in range(2):
                        for q in range(2):
                            n = P * (2 * q + i)
                            last = mm(ps_t[a][:, 256 * i + P * q:256 * i + P * q + P], negpick[:, n:n + P],
                                      mxt[:, b % 2, a, :], start=False)
                    last.then_inc(s_st, 1)

            def values(b):
                if b == 0:
                    pe.wait_ge(s_vbd, 1)
                    pe.wait_ge(s_kbd, 4)
                elif b >= 2:
                    pe.wait_ge(s_at, b - 1)
                pe.wait_ge(s_exp, 2 * b + 2)
                for o, rhs in ((0, None), (256, const_ap("rowsum"))):
                    for i in range(4):
                        lhsT = rhs if rhs is not None else vbd[:, b, 32 * i:32 * i + 32]
                        last = pe.matmul(av_bank[b % 2][32 * i:32 * i + 32, o:o + 256], lhsT, pt[:, b % 2, i, :],
                                         start=(o == 0), stop=True, skip_group_check=True,
                                         tile_position=(0, 32 * i))
                last.then_inc(s_av, 1)

            def outs(b):
                o = out_bank[b]
                pe.wait_ge(s_at, b + 1)
                pe.wait_ge(s_xc, b // 2 + 1)
                if b == 0:
                    pe.wait_ge(s_g, 1)
                    pe.wait_ge(s_rows, 2)
                elif b == 1:
                    pe.wait_ge(s_u, 2)
                else:
                    pe.wait_ge(s_mxt, 8)
                for par in range(2):
                    mm(o[:, 256 * par:256 * par + 256], at[:, b % 2, par], mo_g, start=(par == 0), stop=False)
                    last = mm(o[:, 256 * par + C:256 * par + 2 * C], xc[:, 2 * b + par, :], wmlp, start=False)
                last.then_inc(s_out, 1)

            def sums(g, par):
                if g == 0 and par == 0:
                    pe.wait_ge(s_vm, 1)
                elif g == 1 and par == 1:
                    pe.wait_ge(s_at, 3)
                else:
                    pe.wait_ge(s_exp, 8)
                for b in range(2):
                    pe.wait_ge(s_x1, 2 * g + b + 1)
                    last = mm(mix_bank[g][par][:, P * b:P * b + P], x1[:, 4 * g + 2 * b + par, :], wsd[:, par, :],
                              start=(b == 0))
                last.then_inc(s_ctps[par], 1)

            def layer1(g, par):
                pe.wait_ge(s_ct[par], g + 1)
                na, nf = PAIRS[par], FIXED[par]
                o = mix_bank[g][par][:, 256:512].rearrange("p (b n) -> p b n", b=2)
                src = ct[:, g, par]
                mm(o[:, :, 0:na + nf], w0, src[:, :, 0:na + nf], start=True, stop=False)
                mm(o[:, :, na + nf:P], w0, src[:, :, 0:na], start=False, stop=False)
                mm(o[:, :, 0:na], w1, src[:, :, na + nf:P], start=False)
                mm(o[:, :, na + nf:P], nw1[:], src[:, :, na + nf:P], start=False).then_inc(s_tps[par], 1)

            def layer2(g, par):
                na, nf = PAIRS[par], FIXED[par]
                o = mix_bank[g][par][:, 0:256].rearrange("p (b n) -> p b n", b=2)
                pe.wait_ge(s_o1k[par], g + 1)
                pe.wait_ge(s_o1n[par], g + 1)
                mm(o, wk, o1k[:, g, par], start=True, stop=False)
                src = o1n[:, g, par]
                if nf:
                    mm(o[:, :, na:na + nf], wn, src[:, :, na:na + nf], start=False)
                mm(o[:, :, 0:na], wn, src[:, :, na + nf:P], start=False)
                mm(o[:, :, na + nf:P], wn, src[:, :, 0:na], start=False).then_inc(s_yps[par], 1)

            def back_c(g, par):
                pe.wait_ge(s_ys[par], g + 1)
                for b in range(2):
                    last = mm(mix_bank[g][par][:, 256 + P * b:256 + P * b + P], ys[:, g, par, b, :], cas,
                              start=(b == 0))
                last.then_inc(s_ydps[par], 1)

            def back_w(g, par):
                pe.wait_ge(s_yd[par], g + 1)
                mm(mix_bank[g][par][:, 0:256], winv[:, par, :], yd[:, g, par].rearrange("p b n -> p (b n)")
                   ).then_inc(s_fps[par], 1)

            scores_q(0)
            scores_k(0, 0)
            scores_k(0, 1)
            turn_max(0)
            for b in range(3):
                shift(b)
                scores_q(b + 1)
                if b >= 1:
                    values(b - 1)
                if b == 2:
                    outs(0)
                scores_k(b + 1, 0)
                turn_max(b + 1)
                scores_k(b + 1, 1)
            shift(3)
            values(2)
            outs(1)
            values(3)
            outs(2)
            sums(0, 0)
            sums(0, 1)
            outs(3)
            for step, g, par in MIX_ORDER:
                (layer1, layer2, back_c, back_w, sums)[step](g, par)


def lay_out(x, i):
    f = np.ascontiguousarray
    x = np.asarray(x)
    x_tok = f(x.reshape(TILES, P, C).transpose(1, 0, 2))
    xr = x.reshape(B, 8, 2, 8, 2, C)
    x_par = f(xr.transpose(4, 1, 3, 0, 2, 5).reshape(P, TILES, C))
    x_chan = f(xr.transpose(5, 0, 2, 4, 1, 3).reshape(C, TILES, P))
    vecs = {"ln_g": i["L0_conv_ln_g"], "ln_b": i["L0_conv_ln_b"], "dw_b": i["L0_conv_dw_b"],
            "bq": i["L0_conv_bq"], "bv": i["L0_conv_bv"], "mq_b": i["L0_conv_mq_b"],
            "mk_b": i["L0_conv_mk_b"], "mv_b": i["L0_conv_mv_b"], "mo_b": i["L0_conv_mo_b"],
            "mlp_b": i["L0_conv_mlp_b"],
            "b1k": i["L1_conv_b1"][0], "b1n": i["L1_conv_b1"][1], "b2k": i["L1_conv_b2"][0],
            "b2n": i["L1_conv_b2"][1], "pw0": i["L0_conv_pw_w"][0], "pw1": i["L0_conv_pw_w"][1]}
    vecs = {n: np.asarray(v).reshape(C) for n, v in vecs.items()}
    image = lambda a: a.reshape(*a.shape[:-1], 8, 8, 2).swapaxes(-1, -2).reshape(a.shape)
    vecs["bq_img"] = image(vecs["bq"])
    early = np.concatenate([image(i["L0_conv_wq"]), i["L0_conv_dw_w"].reshape(C, NTAP),
                            np.stack([vecs[n] for n in VECTORS], axis=1)], axis=1)
    w1 = i["L1_conv_w1"].transpose(1, 2, 0, 3).reshape(C, 32)
    w2 = i["L1_conv_w2"].transpose(1, 2, 0, 3).reshape(C, 32)
    w2t = i["L1_conv_w2"].transpose(1, 3, 0, 2).reshape(C, 32)
    late = np.concatenate([i["L0_conv_wq"].T, i["L0_conv_mq_w"], i["L0_conv_wv"].T, i["L0_conv_mk_w"],
                           i["L0_conv_mv_w"], i["L0_conv_mo_w"].T, i["L0_conv_mlp_w"], w1, w2, w2t,
                           i["L0_conv_mo_w"]], axis=1)
    rows = np.concatenate([vecs[n] for n in ROWS])[None]
    return {"x_tok": x_tok, "x_par": x_par, "x_chan": x_chan, "early": f(early), "late": f(late),
            "rows": f(rows), "const": constants(), "pick": picks()}


def kernel(**inputs):
    import concourse.bacc as bacc
    from concourse.bass_utils import run_bass_kernel_spmd as run

    inputs = {n: np.asarray(v) for n, v in inputs.items()}
    arrays = lay_out(inputs["x"], inputs)
    nc = bacc.Bacc("TRN2", target_bir_lowering=False, num_devices=1)
    args = [nc.dram_tensor(f"in_{n}", a.shape, F32, kind="ExternalInput").ap() for n, a in arrays.items()]
    out = nc.dram_tensor("out_tiles", (P, TILES, C), F32, kind="ExternalOutput").ap()
    build(nc, *args, out)
    r = run(nc, [{f"in_{n}": a for n, a in arrays.items()}], core_ids=[0])
    o = np.asarray(r.results[0]["out_tiles"]).reshape(2, 8, 8, B, 2, C)
    return np.ascontiguousarray(o.transpose(3, 1, 4, 2, 0, 5).reshape(B, H, W, C))
```

```python
from contextlib import ExitStack

import numpy as np

import concourse.bass as bass
from concourse import mybir

ALU = mybir.AluOpType
ACT = mybir.ActivationFunctionType
F32 = mybir.dt.float32
F32R = mybir.dt.float32r
AX_X = mybir.AxisListType.X

B, H, W, C = 4, 16, 16, 128
P = 128
HEADS, HD = 8, 16
KS, PAD, R = 7, 3, 2
HG = H // R
KEYS = HG * HG
TILES = B * 2
EPS = 1e-5
SPARSITY = 0.01
COORD = 4.0 * 0.5 * (W - 1)

def tile_tokens(par):
    return [(2 * h2 + par, 2 * w2 + half) for half in range(2) for h2 in range(8) for w2 in range(8)]


def frequency_pairs(par):
    first, fixed, second, seen = [], [], [], set()
    for h in range(par, H, 2):
        for v in range(W):
            a, b = (h, v), ((-h) % H, (-v) % W)
            if a in seen:
                continue
            seen |= {a, b}
            if a == b:
                fixed.append(a)
            else:
                first.append(a)
                second.append(b)
    return first, fixed, second


PAIRS = [len(frequency_pairs(par)[0]) for par in range(2)]
FIXED = [len(frequency_pairs(par)[1]) for par in range(2)]
SUMS = max(n + f for n, f in zip(PAIRS, FIXED))

CONST_W = {"ident": P, "wsd": 4 * SUMS, "winv": 2 * P, "cas": P, "center": P, "dist": 2 * KEYS, "lower": 1,
           "vmask": P, "rowsum": 32, "block": 8, "half": 8}
CONST = {}
_at = 0
for _name, _w in CONST_W.items():
    CONST[_name] = (_at, _at + _w)
    _at += _w
CONST_N = _at

VECTORS = ["ln_g", "ln_b", "dw_b", "bq", "bv", "mq_b", "mk_b", "mv_b", "b2n", "mo_b", "b1k", "b1n",
           "b2k", "pw0", "pw1"]
VEC = {n: i for i, n in enumerate(VECTORS)}
NTAP = KS * KS
EARLY_N = P + NTAP + len(VECTORS)
WEIGHTS = ["wqT", "mq", "wvT", "mk", "mv", "moT", "mlp"]
LATE = {n: (i * P, (i + 1) * P) for i, n in enumerate(WEIGHTS)}
_at = len(WEIGHTS) * P
for _name in ("w1", "w2", "w2T"):
    LATE[_name] = (_at, _at + 32)
    _at += 32
LATE["mo"] = (_at, _at + P)
LATE_N = _at + P
ROWS = ["ln_g", "ln_b", "bq_img", "mlp_b"]


def constants():
    c = {}
    eye = np.eye(P)
    c["ident"] = eye

    def cas(n):
        t = np.arange(n)
        a = 2.0 * np.pi * (np.outer(t, t) % n) / n
        return np.cos(a) + np.sin(a)

    cw = cas(W)
    wsd, winv = np.zeros((P, 2, 2 * SUMS)), np.zeros((P, 2, P))
    for par in range(2):
        first, fixed, second = frequency_pairs(par)
        for row, (h, w) in enumerate(tile_tokens(par)):
            for n, (fh, fv) in enumerate(first + fixed):
                gh, gv = (-fh) % H, (-fv) % W
                s = cw[fv, w] * (fh == h) + cw[gv, w] * (gh == h)
                d = cw[fv, w] * (fh == h) - cw[gv, w] * (gh == h)
                wsd[row, par, n] = 0.5 * s
                if n < len(first):
                    wsd[row, par, len(first) + len(fixed) + n] = 0.5 * d
            for n, (fh, fv) in enumerate(first + fixed + second):
                winv[n, par, row] = cw[fv, w] * (fh == h) / (W * C)
    c["wsd"], c["winv"], c["cas"] = wsd, winv, cas(C)
    c["center"] = eye - 1.0 / C
    p = np.arange(P)[:, None]
    i, j = np.arange(KEYS)[None] // HG, np.arange(KEYS)[None] % HG
    dist = np.zeros((P, 2, KEYS))
    dist[:, 0] = (j + 1.5) * 0.5 * (W - 1) - p % W
    dist[:, 1] = (i + 1.5) * 0.5 * (W - 1) - p // W
    c["dist"] = dist
    c["lower"] = np.full((P, 1), -(H // 2))
    head = np.arange(P) // HD
    which = np.arange(P) // KEYS
    c["vmask"] = (head[None] % 2 == which[:, None]) * 1.0
    c["rowsum"] = c["vmask"][:, :32]
    c["block"] = (head[:, None] == np.arange(8)[None]) * 1.0
    c["half"] = 0.5 * c["block"]
    return np.concatenate([c[n].reshape(P, -1) for n in CONST_W], axis=1).astype(np.float32)


def picks():
    return np.kron(np.eye(HEADS), np.ones(KEYS)).astype(np.float32)


def reach(k):
    outs = [o for o in range(HG) if 0 <= R * o + k - PAD < H]
    return outs[0], len(outs), R * outs[0] + k - PAD


ALL_TAPS = sorted(((kh, kw) for kh in range(KS) for kw in range(KS)),
                  key=lambda t: -reach(t[0])[1] * reach(t[1])[1])
PE_TAPS = [(3, 3)] + [t for t in ALL_TAPS[3:] if t != (3, 3)][-23:]
FB_AT, OB_AT = 4, 8
OB_PS_AT = 5
XN_AT = (1, 3, 6, 7)
CENTER_AT = 12
DVE_TAPS = [t for t in ALL_TAPS if t not in PE_TAPS]


def build(nc, x_tok, x_chan, early, late, rows, const, pick, out):
    with ExitStack() as ctx:
        def sb(name, shape, dt=F32):
            return ctx.enter_context(nc.sbuf_tensor(name, shape, dt))

        def sem(name):
            return ctx.enter_context(nc.semaphore(name))

        xt = sb("xt", [P, TILES, C])
        xc = sb("xc", [C, TILES, P])
        xch = sb("xch", [C, TILES, P], F32R)
        xcl = sb("xcl", [C, TILES, P], F32R)
        ew = sb("ew", [P, EARLY_N])
        lw = sb("lw", [P, LATE_N + P])
        rb = sb("rb", [P, len(ROWS), C])
        cs = sb("cs", [P, CONST_N])
        ones = sb("ones", [P, P])
        pk = sb("pk", [8, 4 * P])
        negpick = sb("negpick", [8, 4 * P], F32R)
        mhalf = sb("mhalf", [P, TILES])
        spare0 = sb("spare0", [P, 1])
        spare = sb("spare", [P, 4])
        stats = sb("stats", [P, TILES, 6])
        mv = sb("mv", [P, TILES, 2])
        vareps = sb("vareps", [P, TILES])
        rstd = sb("rstd", [P, TILES])
        nmr = sb("nmr", [P, B])
        xn = sb("xn", [P, TILES, C])
        xg = sb("xg", [P, TILES, C])
        xl = sb("xl", [P, TILES, C])
        qbias = sb("qbias", [C, P])
        q_img = sb("q_img", [C, H, 2, W // 2, B])
        diag = sb("diag", [C, len(PE_TAPS), P])
        acc = sb("acc", [C, 2, HG, HG * B])
        accs = sb("accs", [C, KEYS * B])
        conv = sb("conv", [C, KEYS, B])
        og = sb("og", [C, B, KEYS])
        pwb = sb("pwb", [C, 2, P])
        th = sb("th", [P, 2, B, KEYS])
        dist = sb("dist", [P, 2, B, KEYS])
        absd = sb("absd", [P, 3, B, KEYS])
        hat = sb("hat", [P, 3, B, KEYS])
        wt = sb("wt", [P, 2, B, KEYS])
        it = sb("it", [C, B, 2, KEYS])
        gmlp = sb("gmlp", [C, C])
        fw = sb("fw", [C, 4, C])
        iw = sb("iw", [C, 3 * C], F32R)
        fb = sb("fb", [C, 4])
        bd1 = sb("bd1", [C, 2, 8, 16])
        ab = sb("ab", [C, 4, 16])
        abd = sb("abd", [C, 4, 8, 16])
        m1 = sb("m1", [C, C])
        fl = sb("fl", [C, 4, C])
        ob = sb("ob", [C, 1])
        ksb = sb("ksb", [C, B, KEYS])
        mlp_row = sb("mlp_row", [P, C])
        qh = sb("qh", [C, B, 2, P])
        qhr = sb("qhr", [C, B, 2, P], F32R)
        qlo = sb("qlo", [C, B, 2, P], F32R)
        kbd = sb("kbd", [C, B, HEADS, KEYS])
        kbr = sb("kbr", [C, B, HEADS, KEYS], F32R)
        klo = sb("klo", [C, B, HEADS, KEYS], F32R)
        vbd = sb("vbd", [P, B, C])
        mx = sb("mx", [P, 2, 2, HEADS])
        pt = sb("pt", [P, 2, 4, 2 * P])
        rs = sb("rs", [C, 2, 2 * P])
        at = sb("at", [C, 2, 2, P])
        mxt = sb("mxt", [HEADS, 2, 2 * P], F32R)
        stats2 = sb("stats2", [P, TILES, 6])
        mv2 = sb("mv2", [P, TILES, 2])
        vareps2 = sb("vareps2", [P, TILES])
        rstd2 = sb("rstd2", [P, TILES])
        um = sb("um", [P, 4, C])
        u = sb("u", [P, TILES, C])
        ug = sb("ug", [P, TILES, C])
        x1 = sb("x1", [P, TILES, C])
        ct = sb("ct", [C, 2, 2, 2, 2 * SUMS])
        rd = sb("rd", [C, 2, 2, 2, SUMS])
        pm = sb("pm", [C, 2, 2, 2, P])
        o1k = sb("o1k", [C, 2, 2, 2, P])
        o1n = sb("o1n", [C, 2, 2, 2, P])
        yc = sb("yc", [C, 2, 2, 2, P])
        ys = sb("ys", [C, 2, 2, 2, P])
        yd = sb("yd", [P, 2, 2, 2, C])
        lim = sb("lim", [C, 2])
        fin = sb("fin", [P, TILES, C])

        bank = [ctx.enter_context(nc.psum_tensor(f"bank{i}", [P, 512], F32)) for i in range(8)]
        ps_s = bank[0:2]
        ps_t = bank[2:4]
        ps_av = bank[4]
        ps_out = bank[5]
        ps_mix = bank[6:8]

        av_bank = (ps_av, ps_mix[0])
        turn_bank = (ps_av, ps_mix[1], ps_mix[1], ps_mix[1])
        out_bank = (ps_out, ps_mix[1], ps_s[0], ps_s[1])
        mix_bank = ((ps_t[0], ps_t[1]), (ps_av, ps_mix[0]))

        def const_ap(name):
            return cs[:, CONST[name][0]:CONST[name][1]]

        def late_ap(name):
            return lw[:, LATE[name][0]:LATE[name][1]]

        def vec(name):
            i = P + NTAP + VEC[name]
            return ew[:, i:i + 1]

        wq = ew[:, 0:P]
        ident, cas = const_ap("ident"), const_ap("cas")
        wsd = const_ap("wsd").rearrange("p (a n) -> p a n", a=2)
        winv = const_ap("winv").rearrange("p (a n) -> p a n", a=2)
        dconst = const_ap("dist").rearrange("p (a n) -> p a n", a=2)
        block8, half8 = const_ap("block"), const_ap("half")
        mo_g = lw[:, LATE["mo"][0]:LATE["mo"][0] + 2 * P]
        wqq, wvk, wvv, wmlp = (fw[:, i, :] for i in range(4))
        w0, w1, wk, wn = (fl[:, i, :] for i in range(4))

        d_x, d_early, d_rows, d_ident, d_const, d_late, d_xc, d_pick, d_out = (
            sem("d_" + n) for n in ("x0", "early", "rows", "ident", "const", "late", "xc", "pick", "out"))
        d_x = [d_x] + [sem(f"d_x{b}") for b in range(1, B)]
        s_ones, s_mhalf, s_spare = sem("s_ones"), sem("s_mhalf"), sem("s_spare")
        s_stats, s_mv, s_var, s_rstd = sem("s_stats"), sem("s_mv"), sem("s_var"), sem("s_rstd")
        s_nmr, s_xn, s_xn1, s_xg, s_xl = sem("s_nmr"), sem("s_xn"), sem("s_xn1"), sem("s_xg"), sem("s_xl")
        s_colsum, s_qbias, s_qps, s_qimg = sem("s_colsum"), sem("s_qbias"), sem("s_qps"), sem("s_qimg")
        s_diag, s_acc, s_accs = sem("s_diag"), [sem("s_acc0"), sem("s_acc1")], sem("s_accs")
        s_convps, s_conv, s_og = sem("s_convps"), sem("s_conv"), sem("s_og")
        s_pwb, s_gmlp, s_bd1, s_ab, s_abd = (sem("s_" + n) for n in ("pwb", "gmlp", "bd1", "ab", "abd"))
        s_fwps, s_fw, s_fbps, s_fb, s_m1 = (sem("s_" + n) for n in ("fwps", "fw", "fbps", "fb", "m1"))
        s_gps, s_g, s_rows, s_flps, s_fl = (sem("s_" + n) for n in ("gps", "g", "rows", "flps", "fl"))
        s_xc, s_lim, s_obps, s_ob, s_fb3ps, s_fb3, s_ksb, s_iw, s_iwl, s_xch, s_xcl, s_qlo, s_klo, s_negpick = (sem("s_" + n) for n in ("xc", "lim", "obps", "ob", "fb3ps", "fb3", "ksb", "iw", "iwl", "xch", "xcl", "qlo", "klo", "negid"))
        s_qhps, s_qh, s_qh2 = sem("s_qhps"), sem("s_qh"), sem("s_qh2")
        s_off, s_th, s_dist, s_abs, s_hat, s_wt = (
            sem("s_" + n) for n in ("off", "th", "dist", "abs", "hat", "wt"))
        s_itps, s_it, s_kps, s_kbd0, s_kbd, s_kbr0, s_kbr, s_vps, s_vbd = (
            sem("s_" + n) for n in ("itps", "it", "kps", "kbd0", "kbd", "kbr0", "kbr", "vps", "vbd"))
        s_mxtps, s_mxt = sem("s_mxtps"), sem("s_mxt")
        s_s, s_mx, s_st, s_exp, s_av, s_rs, s_at = (
            sem("s_" + n) for n in ("s", "mx", "st", "exp", "av", "rs", "at"))
        s_out, s_stats2, s_mv2, s_var2, s_rstd2, s_um, s_u, s_u2, s_ug, s_x1 = (
            sem("s_" + n) for n in ("out", "stats2", "mv2", "var2", "rstd2", "um", "u", "u2", "ug", "x1"))
        s_ctps, s_ct, s_tps, s_rd, s_pm, s_o1, s_yps, s_yc, s_ys, s_ydps, s_yd, s_fps, s_fin = (
            [sem(f"s_{n}{par}") for par in range(2)]
            for n in ("ctps", "ct", "tps", "rd", "pm", "o1", "yps", "yc", "ys", "ydps", "yd", "fps", "fin"))

        def window(kh, kw):
            oh, nh, ih = reach(kh)
            ow, nw, iw = reach(kw)
            src = q_img[:, ih:ih + R * nh - 1:R, iw % 2, iw // 2:iw // 2 + nw, :].rearrange("c h w b -> c h (w b)")
            return src, slice(oh, oh + nh), slice(B * ow, B * (ow + nw))

        def tap(kh, kw):
            i = P + kh * KS + kw
            return ew[:, i:i + 1]

        def halves(g, par):
            n = 2 * (PAIRS[par] + FIXED[par])
            o = mix_bank[g][par][:, 512 - 2 * n:512].rearrange("p (a b n) -> p a b n", a=2, b=2)
            return o[:, 0], o[:, 1]

        block = ctx.enter_context(nc.Block())

        @block.sync
        def _(sp):
            for b in range(B):
                sp.dma_start(xt[:, 2 * b:2 * b + 2, :], x_tok[:, 2 * b:2 * b + 2, :]).then_inc(d_x[b], 16)
            sp.dma_start(rb[:].rearrange("p a n -> p (a n)"), rows.broadcast_to([P, len(ROWS) * C])).then_inc(d_rows, 16)
            sp.dma_start(lw[:, 0:LATE_N], late).then_inc(d_late, 16)
            sp.dma_start(cs[:, P:CONST_N], const[:, P:CONST_N]).then_inc(d_const, 16)
            sp.dma_start(pk[:], pick).then_inc(d_pick, 16)
            sp.dma_start(xc[:], x_chan).then_inc(d_xc, 16)
            for g in range(2):
                for par in range(2):
                    sp.wait_ge(s_fin[par], g + 1)
                    sp.dma_start(out[:, 4 * g + par:4 * g + par + 3:2, :],
                                 fin[:, 4 * g + par:4 * g + par + 3:2, :]).then_inc(d_out, 16)
            sp.wait_ge(d_out, 64)

        @block.gpsimd
        def _(pool):
            pool.memset(ones[:], 1.0).then_inc(s_ones, 1)
            pool.memset(spare0[:], 0.0).then_inc(s_spare, 1)
            pool.memset(mhalf[:], -0.5).then_inc(s_mhalf, 1)
            pool.wait_ge(s_mhalf, 1)
            for b in range(B):
                pool.wait_ge(s_var, b + 1)
                pool.tensor_tensor(rstd[:, 2 * b:2 * b + 2], vareps[:, 2 * b:2 * b + 2], mhalf[:, 0:2],
                                   ALU.pow).then_inc(s_rstd, 1)
            pool.wait_ge(d_rows, 16)
            for g in range(2):
                pool.wait_ge(s_xn, 2 * g + 2)
                pool.wait_ge(s_xn1, 2 * g + 2)
                t = slice(4 * g, 4 * g + 4)
                pool.tensor_tensor(xg[:, t, :], xn[:, t, :], rb[:, 0:1, :].broadcast_to([P, 4, C]),
                                   ALU.mult).then_inc(s_xg, 1)
                pool.wait_ge(s_xg, g + 1)
                pool.tensor_tensor(xl[:, t, :], xg[:, t, :], rb[:, 1:2, :].broadcast_to([P, 4, C]),
                                   ALU.add).then_inc(s_xl, 1)
            pool.wait_ge(d_xc, 16)
            pool.wait_ge(s_ob, 1)
            tiles = [slice(4 * g, 4 * g + 4) for g in range(2)]
            for t in tiles:
                pool.tensor_tensor(xc[:, t, :], xc[:, t, :], ob[:].unsqueeze(1).broadcast_to([C, 4, P]),
                                   ALU.add).then_inc(s_xc, 1)
            pool.wait_ge(d_late, 16)
            for i, name in enumerate(("w2", "w2T")):
                a = lw[:, LATE[name][0]:LATE[name][0] + 16]
                b = lw[:, LATE[name][0] + 16:LATE[name][1]]
                pool.tensor_tensor(ab[:, 2 * i, :], a, b, ALU.add).then_inc(s_ab, 1)
                pool.tensor_tensor(ab[:, 2 * i + 1, :], a, b, ALU.subtract).then_inc(s_ab, 1)
            pool.wait_ge(d_const, 16)
            for i in range(2):
                w = lw[:, LATE["w1"][0] + 16 * i:LATE["w1"][0] + 16 * i + 16]
                pool.tensor_tensor(bd1[:, i], w.unsqueeze(1).broadcast_to([C, 8, 16]),
                                   block8.unsqueeze(2).broadcast_to([C, 8, 16]), ALU.mult).then_inc(s_bd1, 1)
            pool.wait_ge(s_ab, 4)
            for i in range(4):
                pool.tensor_tensor(abd[:, i], ab[:, i, :].unsqueeze(1).broadcast_to([C, 8, 16]),
                                   half8.unsqueeze(2).broadcast_to([C, 8, 16]), ALU.mult).then_inc(s_abd, 1)
            pool.wait_ge(s_abd, 4)
            pool.wait_ge(d_ident, 16)
            pool.tensor_tensor(m1[:], ident, abd[:, 1].rearrange("p a n -> p (a n)"), ALU.add).then_inc(s_m1, 1)
            def low(dst, whole, high, done):
                pool.tensor_tensor(dst, whole, high.bitcast(F32), ALU.subtract).then_inc(done, 1)

            pool.wait_ge(s_iw, 2)
            low(iw[:, 2 * C:3 * C], wmlp, iw[:, C:2 * C], s_iwl)
            for g, t in enumerate(tiles):
                pool.wait_ge(s_xch, g + 1)
                low(xcl[:, t, :], xc[:, t, :], xch[:, t, :], s_xcl)
            pool.wait_ge(s_qh, 2)
            low(qlo[:, 0:2], qh[:, 0:2], qhr[:, 0:2], s_qlo)
            pool.wait_ge(s_qh2, 2)
            low(qlo[:, 2:4], qh[:, 2:4], qhr[:, 2:4], s_qlo)

            def keys(b):
                pool.tensor_tensor(kbd[:, b], ksb[:, b:b + 1, :].broadcast_to([C, HEADS, KEYS]),
                                   block8.unsqueeze(2).broadcast_to([C, HEADS, KEYS]), ALU.mult).then_inc(s_kbd, 1)

            def keys_low(b):
                pool.wait_ge(s_kbr, b)
                pool.wait_ge(s_kbd, b)
                low(klo[:, b], kbd[:, b], kbr[:, b], s_klo)

            pool.wait_ge(s_ksb, 1)
            keys(1)
            keys(2)
            keys_low(1)
            keys(3)
            keys_low(2)
            keys_low(3)
            for b in range(B):
                pool.wait_ge(s_var2, b + 1)
                pool.tensor_tensor(rstd2[:, 2 * b:2 * b + 2], vareps2[:, 2 * b:2 * b + 2],
                                   mhalf[:, 0:2], ALU.pow).then_inc(s_rstd2, 1)
                if b < 2:
                    pool.wait_ge(s_rows, 1)
                    pool.wait_ge(s_um, 2 * b + 2)
                    pool.tensor_tensor(u[:, 2 * b:2 * b + 2, :], um[:, 2 * b:2 * b + 2, :],
                                       mlp_row[:].unsqueeze(1).broadcast_to([P, 2, C]), ALU.add).then_inc(s_u, 1)

        @block.scalar
        def _(act):
            act.dma_start(ew[:], early).then_inc(d_early, 16)
            act.dma_start(cs[:, 0:P], const[:, 0:P]).then_inc(d_ident, 16)
            act.wait_ge(s_spare, 1)
            act.activation(spare[:, 2:3], spare0[:, 0:1], ACT.Copy)
            act.wait_ge(d_early, 16)
            act.wait_ge(d_ident, 16)
            for n, (kh, kw) in enumerate(PE_TAPS):
                if n in XN_AT:
                    b = XN_AT.index(n)
                    act.wait_ge(s_nmr, b + 1)
                    act.activation(xn[:, 2 * b + 1, :], xt[:, 2 * b + 1, :], ACT.Identity, bias=nmr[:, b:b + 1],
                                   scale=rstd[:, 2 * b + 1:2 * b + 2]).then_inc(s_xn1, 1)
                act.activation(diag[:, n, :], ident, ACT.Copy, scale=tap(kh, kw)).then_inc(s_diag, 1)
            act.wait_ge(d_late, 16)
            act.activation(gmlp[:], late_ap("mlp"), ACT.Copy, scale=vec("ln_g")).then_inc(s_gmlp, 1)
            for k in range(2):
                act.copy(pwb[:, k, :], vec(f"pw{k}").broadcast_to([C, P])).then_inc(s_pwb, 1)
            act.wait_ge(d_pick, 16)
            act.mul(negpick[:], pk[:], -1.0).then_inc(s_negpick, 1)
            act.wait_ge(s_fwps, 1)
            act.copy(fw[:], ps_mix[0][:].rearrange("p (a n) -> p a n", a=4)).then_inc(s_fw, 1)
            act.copy(iw[:, C:2 * C], ps_mix[0][:, 3 * P:4 * P]).then_inc(s_iw, 1)
            act.copy(iw[:, 0:C], ident).then_inc(s_iw, 1)
            act.activation(spare[:, 0:1], spare0[:, 0:1], ACT.Gelu)
            for g in range(2):
                act.wait_ge(s_xc, g + 1)
                act.copy(xch[:, 4 * g:4 * g + 4, :], xc[:, 4 * g:4 * g + 4, :]).then_inc(s_xch, 1)
            act.wait_ge(s_conv, 1)
            act.activation(og[:], conv[:].rearrange("c n b -> c b n"), ACT.Gelu, bias=vec("dw_b")).then_inc(s_og, 1)
            for n, k in enumerate((1, 0)):
                act.wait_ge(s_off, n + 1)
                act.activation(th[:, k], ps_t[k][:, 0:256].rearrange("p (b n) -> p b n", b=B),
                               ACT.Tanh).then_inc(s_th, 1)
            for i in range(3):
                act.wait_ge(s_dist, min(i, 1) + 1)
                act.activation(absd[:, i], dist[:, min(i, 1)], ACT.Abs,
                               bias=const_ap("lower") if i == 2 else 0.0).then_inc(s_abs, 1)
            act.wait_ge(s_fb, 1)
            act.wait_ge(s_qhps, 2)
            for dst in (qh, qhr):
                act.activation(dst[:, 2:4], ps_out[:].rearrange("p (b a n) -> p b a n", b=2, a=2), ACT.Identity,
                               bias=fb[:, 0:1]).then_inc(s_qh2, 1)
            act.wait_ge(s_flps, 1)
            act.copy(fl[:], ps_mix[1][:].rearrange("p (a n) -> p a n", a=4)).then_inc(s_fl, 1)
            act.wait_ge(s_gps, 1)
            act.copy(lw[:, LATE_N:LATE_N + P], ps_out[:, 0:P]).then_inc(s_g, 1)
            act.activation(spare[:, 1:2], spare0[:, 0:1], ACT.Exp)

            act.wait_ge(s_kps, 2)
            act.activation(ksb[:], ps_t[1][:, 0:256].rearrange("p (b n) -> p b n", b=B), ACT.Identity,
                           bias=fb[:, 1:2]).then_inc(s_ksb, 1)

            def keys(b):
                act.wait_ge(s_kbd, b)
                act.copy(kbr[:, b], kbd[:, b]).then_inc(s_kbr, 1)

            def exp(b):
                if b >= 2:
                    act.wait_ge(s_av, b - 1)
                for a in range(2):
                    act.wait_ge(s_st, 2 * b + a + 1)
                    act.activation(pt[:, b % 2, 2 * a:2 * a + 2, :],
                                   ps_t[a][:].rearrange("p (i n) -> p i n", i=2), ACT.Exp).then_inc(s_exp, 1)

            def mlp_scaled(b):
                act.wait_ge(s_rstd2, b + 1)
                for i in range(2):
                    act.activation(um[:, 2 * b + i, :], out_bank[b][:, 256 * i + C:256 * i + 2 * C], ACT.Copy,
                                   scale=rstd2[:, 2 * b + i:2 * b + i + 1]).then_inc(s_um, 1)

            def gelu(b):
                act.wait_ge(*((s_u, b + 1) if b < 2 else (s_u2, 2 * b - 2)))
                t = slice(2 * b, 2 * b + 2)
                act.activation(ug[:, t, :], u[:, t, :], ACT.Gelu).then_inc(s_ug, 1)

            def sums(g, par):
                act.wait_ge(s_ctps[par], g + 1)
                n = 2 * (PAIRS[par] + FIXED[par])
                act.copy(ct[:, g, par, :, 0:n], mix_bank[g][par][:, 0:2 * n].rearrange("p (b n) -> p b n", b=2)
                         ).then_inc(s_ct[par], 1)

            def turned_max(b):
                if b >= 2:
                    act.wait_ge(s_st, 2 * b - 2)
                act.wait_ge(s_mxtps, b + 1)
                act.copy(mxt[:, b % 2], turn_bank[b][0:HEADS, 0:2 * P]).then_inc(s_mxt, 1)

            def differences(g, par):
                act.wait_ge(s_tps[par], g + 1)
                n = PAIRS[par] + FIXED[par]
                act.copy(rd[:, g, par, :, 0:n], halves(g, par)[1]).then_inc(s_rd[par], 1)

            def relus(g, par):
                act.wait_ge(s_pm[par], 2 * g + 2)
                src = pm[:, g, par]
                act.activation(o1k[:, g, par], src, ACT.Relu, bias=vec("b1k")).then_inc(s_o1[par], 1)
                act.activation(o1n[:, g, par], src, ACT.Relu, bias=vec("b1n")).then_inc(s_o1[par], 1)

            def back(g, par):
                act.wait_ge(s_ydps[par], g + 1)
                act.copy(yd[:, g, par], mix_bank[g][par][:, 256:512].rearrange("p (b n) -> p b n", b=2)
                         ).then_inc(s_yd[par], 1)

            keys(1)
            turned_max(0)
            keys(2)
            exp(0)
            keys(3)
            turned_max(1)
            exp(1)
            turned_max(2)
            exp(2)
            turned_max(3)
            exp(3)
            mlp_scaled(0)
            gelu(0)
            mlp_scaled(1)
            gelu(1)
            sums(0, 0)
            sums(0, 1)
            gelu(2)
            differences(0, 0)
            gelu(3)
            differences(0, 1)
            relus(0, 0)
            sums(1, 0)
            sums(1, 1)
            relus(0, 1)
            differences(1, 0)
            differences(1, 1)
            relus(1, 0)
            relus(1, 1)
            back(0, 0)
            back(0, 1)
            back(1, 0)
            back(1, 1)

        @block.vector
        def _(dve):
            def statistics(b):
                dve.wait_ge(d_x[b], 16)
                for i in (2 * b, 2 * b + 1):
                    dve.bn_stats(stats[:, i, :], xt[:, i, :]).then_inc(s_stats, 1)
                for i in (2 * b, 2 * b + 1):
                    dve.wait_ge(s_stats, i + 1)
                    dve.bn_aggr(mv[:, i, :], stats[:, i, :]).then_inc(s_mv, 1)
                dve.wait_ge(s_mv, 2 * b + 2)
                dve.tensor_scalar(vareps[:, 2 * b:2 * b + 2], mv[:, 2 * b:2 * b + 2, 1], EPS, None,
                                  ALU.add).then_inc(s_var, 1)

            def normalise(b):
                i = 2 * b
                dve.wait_ge(s_rstd, b + 1)
                dve.scalar_tensor_tensor(out=nmr[:, b:b + 1], in0=mv[:, i + 1, 0:1], scalar=-1.0,
                                         in1=rstd[:, i + 1:i + 2], op0=ALU.mult, op1=ALU.mult).then_inc(s_nmr, 1)
                dve.tensor_scalar(xn[:, i, :], xt[:, i, :], mv[:, i, 0:1], rstd[:, i:i + 1],
                                  ALU.subtract, ALU.mult).then_inc(s_xn, 1)

            statistics(0)
            statistics(1)
            normalise(0)
            statistics(2)
            normalise(1)
            statistics(3)
            dve.wait_ge(s_colsum, 1)
            dve.wait_ge(d_rows, 16)
            dve.wait_ge(d_early, 16)
            dve.scalar_tensor_tensor(out=qbias[:], in0=ps_t[0][:, 0:P], scalar=vec("ln_b"),
                                     in1=rb[:, 2, :], op0=ALU.mult, op1=ALU.add).then_inc(s_qbias, 1)
            normalise(2)
            normalise(3)
            dve.wait_ge(s_qbias, 1)
            for g in range(2):
                dve.wait_ge(s_qps, g + 1)
                for a in range(2):
                    dve.scalar_tensor_tensor(
                        out=q_img[:, 8 * a:8 * a + 8, :, :, 2 * g:2 * g + 2].rearrange("c h p w b -> c b (h p w)"),
                        in0=ps_s[g][:].rearrange("c (b a n) -> c a b n", b=2, a=2)[:, a], scalar=vec("ln_g"),
                        in1=qbias[:].unsqueeze(1).broadcast_to([C, 2, P]),
                        op0=ALU.mult, op1=ALU.add).then_inc(s_qimg, 1)
            dve.wait_ge(s_qimg, 4)
            taps = [0, 0]
            for n, (kh, kw) in enumerate(DVE_TAPS):
                src, oh, ow = window(kh, kw)
                last = n == len(DVE_TAPS) - 1
                a = 0 if last else (len(DVE_TAPS) - n) % 2
                if n == FB_AT:
                    dve.wait_ge(s_fbps, 1)
                    i = P + NTAP + VEC["mq_b"]
                    dve.tensor_tensor(fb[:, 0:3], ps_mix[1][:, 0:3], ew[:, i:i + 3], ALU.add).then_inc(s_fb, 1)
                if n == OB_AT:
                    dve.wait_ge(s_obps, 1)
                    dve.tensor_tensor(ob[:], ps_mix[1][:, 0:1], vec("mo_b"), ALU.add).then_inc(s_ob, 1)
                if last:
                    dve.wait_ge(s_convps, 1)
                    dve.wait_ge(s_acc[1], taps[1])
                    dve.tensor_tensor(accs[:], ps_t[1][:, 0:256], acc[:, 1].rearrange("c h w -> c (h w)"),
                                      ALU.add).then_inc(s_accs, 1)
                dst = acc[:, a, oh, ow]
                if n < 2:
                    dve.tensor_scalar(dst, src, tap(kh, kw), None, ALU.mult).then_inc(s_acc[a], 1)
                else:
                    dve.wait_ge(s_acc[a], taps[a])
                    dve.scalar_tensor_tensor(out=dst, in0=src, scalar=tap(kh, kw), in1=dst, op0=ALU.mult,
                                             op1=ALU.add).then_inc(s_acc[a], 1)
                taps[a] += 1
            dve.wait_ge(s_accs, 1)
            dve.wait_ge(s_acc[0], taps[0])
            dve.tensor_tensor(conv[:].rearrange("c n b -> c (n b)"), acc[:, 0].rearrange("c h w -> c (h w)"),
                              accs[:], ALU.add).then_inc(s_conv, 1)
            dve.wait_ge(s_fb3ps, 1)
            dve.tensor_tensor(fb[:, 3:4], ps_mix[1][:, 0:1], vec("b2n"), ALU.add).then_inc(s_fb3, 1)
            dve.wait_ge(s_fb3, 1)
            dve.tensor_scalar(lim[:, 0:1], fb[:, 3:4], -1.0, -SPARSITY, ALU.mult, ALU.add).then_inc(s_lim, 1)
            dve.tensor_scalar(lim[:, 1:2], fb[:, 3:4], -1.0, SPARSITY, ALU.mult, ALU.add).then_inc(s_lim, 1)
            dve.wait_ge(s_qhps, 1)
            for dst in (qh, qhr):
                dve.tensor_scalar(dst[:, 0:2], ps_av[:].rearrange("p (b a n) -> p b a n", b=2, a=2), fb[:, 0:1], None,
                                  ALU.add).then_inc(s_qh, 1)
            for i, k in enumerate((1, 0)):
                dve.wait_ge(s_th, i + 1)
                dve.scalar_tensor_tensor(out=dist[:, i], in0=th[:, k], scalar=COORD,
                                         in1=dconst[:, i:i + 1, :].broadcast_to([P, B, KEYS]),
                                         op0=ALU.mult, op1=ALU.add).then_inc(s_dist, 1)
            for i in range(3):
                dve.wait_ge(s_abs, i + 1)
                dve.tensor_scalar(hat[:, i], absd[:, i], -1.0, 0.0, ALU.add, ALU.min).then_inc(s_hat, 1)
                if i >= 1:
                    dve.wait_ge(s_hat, i + 1)
                    dve.tensor_tensor(wt[:, i - 1], hat[:, 0], hat[:, i], ALU.mult).then_inc(s_wt, 1)
            dve.wait_ge(s_itps, 1)
            dve.tensor_copy(it[:, :, 0, :], ps_mix[0][:, 0:256].rearrange("p (b n) -> p b n", b=B)).then_inc(s_it, 1)
            dve.wait_ge(s_it, 1)
            dve.tensor_copy(it[:, :, 1, :], it[:, :, 0, :]).then_inc(s_it, 1)
            dve.wait_ge(s_gps, 1)
            dve.wait_ge(s_g, 1)
            dve.tensor_tensor(mlp_row[:], ps_out[:, P:2 * P], rb[:, 3, :], ALU.add).then_inc(s_rows, 1)

            def row_max(b):
                if b >= 2:
                    dve.wait_ge(s_mxtps, b - 1)
                for q in range(2):
                    dve.wait_ge(s_s, 2 * b + q + 1)
                    dve.tensor_reduce(mx[:, b % 2, q], ps_s[q][:].rearrange("p (i n) -> p i n", n=KEYS),
                                      AX_X, ALU.max).then_inc(s_mx, 1)

            def divide(b):
                dve.wait_ge(s_av, b + 1)
                if b >= 2:
                    dve.wait_ge(s_at, b - 1)
                    dve.wait_ge(s_out, b - 1)
                dve.reciprocal(rs[:, b % 2], av_bank[b % 2][:, 256:512]).then_inc(s_rs, 1)
                dve.wait_ge(s_rs, b + 1)
                dve.tensor_tensor(at[:, b % 2].rearrange("c a n -> c (a n)"), av_bank[b % 2][:, 0:256],
                                  rs[:, b % 2], ALU.mult).then_inc(s_at, 1)

            def keys(dst, b, done):
                dve.scalar_tensor_tensor(out=dst[:, b], in0=ps_av[:, KEYS * b:KEYS * b + KEYS].unsqueeze(1)
                                         .broadcast_to([C, HEADS, KEYS]), scalar=fb[:, 1:2],
                                         in1=block8.unsqueeze(2).broadcast_to([C, HEADS, KEYS]), op0=ALU.add,
                                         op1=ALU.mult).then_inc(done, 1)

            dve.wait_ge(s_kps, 1)
            keys(kbr, 0, s_kbr0)
            keys(kbd, 0, s_kbd0)
            row_max(0)
            dve.wait_ge(s_vps, 1)
            dve.tensor_tensor(vbd[:], ps_mix[1][:].rearrange("p (b n) -> p b n", b=B),
                              const_ap("vmask").unsqueeze(1).broadcast_to([P, B, C]), ALU.mult).then_inc(s_vbd, 1)

            def z(b, i=None):
                a = out_bank[b][:].rearrange("p (i n) -> p i n", i=2)[:, :, 0:C]
                return a if i is None else a[:, i, :]

            def moments(b):
                t = slice(2 * b, 2 * b + 2)
                dve.wait_ge(s_out, b + 1)
                for i in range(2):
                    dve.bn_stats(stats2[:, 2 * b + i, :], z(b, i)).then_inc(s_stats2, 1)
                for i in (2 * b, 2 * b + 1):
                    dve.wait_ge(s_stats2, i + 1)
                    dve.bn_aggr(mv2[:, i, :], stats2[:, i, :]).then_inc(s_mv2, 1)
                dve.wait_ge(s_mv2, 2 * b + 2)
                dve.tensor_scalar(vareps2[:, t], mv2[:, t, 1], EPS, None, ALU.add).then_inc(s_var2, 1)

            def mlp_in(b):
                dve.wait_ge(s_rstd2, b + 1)
                for i in range(2):
                    dve.scalar_tensor_tensor(out=u[:, 2 * b + i, :], in0=out_bank[b][:, 256 * i + C:256 * i + 2 * C],
                                             scalar=rstd2[:, 2 * b + i:2 * b + i + 1], in1=mlp_row[:],
                                             op0=ALU.mult, op1=ALU.add).then_inc(s_u2, 1)

            def block_out(b):
                t = slice(2 * b, 2 * b + 2)
                dve.wait_ge(s_ug, b + 1)
                dve.tensor_tensor(x1[:, t, :], ug[:, t, :], z(b), ALU.add).then_inc(s_x1, 1)

            def plus_minus(g, par):
                na, nf = PAIRS[par], FIXED[par]
                t, r = halves(g, par)[0], rd[:, g, par, :, 0:na + nf]
                dve.wait_ge(s_rd[par], g + 1)
                dve.tensor_tensor(pm[:, g, par, :, 0:na + nf], t, r, ALU.add).then_inc(s_pm[par], 1)
                dve.tensor_tensor(pm[:, g, par, :, na + nf:P], t[:, :, 0:na], r[:, :, 0:na],
                                  ALU.subtract).then_inc(s_pm[par], 1)

            def threshold(g, par):
                y = mix_bank[g][par][:, 0:256].rearrange("p (b n) -> p b n", b=2)
                dve.wait_ge(s_yps[par], g + 1)
                dve.tensor_scalar(yc[:, g, par], y, lim[:, 0:1], lim[:, 1:2], ALU.max, ALU.min
                                  ).then_inc(s_yc[par], 1)
                dve.wait_ge(s_yc[par], g + 1)
                dve.tensor_tensor(ys[:, g, par], y, yc[:, g, par], ALU.subtract).then_inc(s_ys[par], 1)

            def finish(g, par):
                dve.wait_ge(s_fps[par], g + 1)
                t = slice(4 * g + par, 4 * g + par + 3, 2)
                dve.tensor_tensor(fin[:, t, :], mix_bank[g][par][:, 0:256].rearrange("p (b n) -> p b n", b=2),
                                  x1[:, t, :], ALU.add).then_inc(s_fin[par], 1)

            dve.wait_ge(s_lim, 2)
            dve.wait_ge(s_rows, 1)
            row_max(1)
            row_max(2)
            divide(0)
            row_max(3)
            divide(1)
            moments(0)
            divide(2)
            moments(1)
            divide(3)
            moments(2)
            block_out(0)
            block_out(1)
            moments(3)
            mlp_in(2)
            mlp_in(3)
            plus_minus(0, 0)
            block_out(2)
            block_out(3)
            plus_minus(0, 1)
            plus_minus(1, 0)
            plus_minus(1, 1)
            threshold(0, 0)
            threshold(0, 1)
            threshold(1, 0)
            threshold(1, 1)
            finish(0, 0)
            finish(0, 1)
            finish(1, 0)
            finish(1, 1)

        @block.tensor
        def _(pe):
            def mm(o, lhsT, rhs, start=True, stop=True):
                return pe.matmul(o, lhsT, rhs, start=start, stop=stop, skip_group_check=True)

            def warm(bank_, n):
                for _ in range(n):
                    mm(bank_[:, 0:P], ones[:], ones[:])

            pe.wait_ge(s_ones, 1)
            warm(ps_out, 6)
            pe.wait_ge(d_early, 16)
            mm(ps_t[0][:, 0:P], ones[:], wq).then_inc(s_colsum, 1)
            warm(ps_out, 6)
            for g in range(2):
                for i in range(4):
                    pe.wait_ge((s_xn, s_xn1)[i % 2], 2 * g + i // 2 + 1)
                    last = mm(ps_s[g][:, P * i:P * i + P], xn[:, 4 * g + i, :], wq, start=(i == 0))
                last.then_inc(s_qps, 1)
            pe.wait_ge(d_late, 16)
            mm(ps_mix[0][:, 0:P], late_ap("wqT"), late_ap("mq"))
            mm(ps_mix[0][:, P:2 * P], late_ap("wvT"), late_ap("mk"), start=False)
            mm(ps_mix[0][:, 2 * P:3 * P], late_ap("wvT"), late_ap("mv"), start=False)
            mm(ps_mix[1][:, 0:1], late_ap("mq"), vec("bq"))
            mm(ps_mix[1][:, 1:2], late_ap("mk"), vec("bv"), start=False)
            mm(ps_mix[1][:, 2:3], late_ap("mv"), vec("bv"), start=False).then_inc(s_fbps, 1)
            pe.wait_ge(s_qimg, 4)
            cps = ps_t[1][:, 0:256].rearrange("c (h w) -> c h w", h=HG)
            for n, (kh, kw) in enumerate(PE_TAPS):
                src, oh, ow = window(kh, kw)
                if n == CENTER_AT:
                    pe.wait_ge(s_gmlp, 1)
                    pe.wait_ge(d_const, 16)
                    mm(ps_mix[0][:, 3 * P:4 * P], const_ap("center"), gmlp[:], start=False).then_inc(s_fwps, 1)
                if n == OB_PS_AT:
                    pe.wait_ge(s_fb, 1)
                    mm(ps_mix[1][:, 0:1], late_ap("mo"), fb[:, 2:3]).then_inc(s_obps, 1)
                pe.wait_ge(s_diag, n + 1)
                last = mm(cps[:, oh, ow], diag[:, n, :], src, start=(n == 0), stop=(n == len(PE_TAPS) - 1))
            last.then_inc(s_convps, 1)
            pe.wait_ge(s_fw, 1)
            def queries(g):
                pe.wait_ge(s_xl, g + 1)
                for i in range(4):
                    o = (ps_av, ps_out)[g][:, 256 * (i // 2):256 * (i // 2) + 256]
                    last = mm(o.rearrange("p (a m) -> p a m", a=2)[:, :, 64 * (i % 2):64 * (i % 2) + 64], wqq,
                              xl[:, 4 * g + i, :].rearrange("p (h a w) -> p a h w", a=2, w=8), start=(i == 0))
                last.then_inc(s_qhps, 1)

            queries(0)
            pe.wait_ge(s_ob, 1)
            pe.wait_ge(s_m1, 1)
            mm(ps_mix[1][:, 0:1], m1[:], vec("b2k")).then_inc(s_fb3ps, 1)
            pe.wait_ge(s_pwb, 2)
            pe.wait_ge(s_qbias, 1)
            pe.wait_ge(s_og, 1)
            for k in (1, 0):
                mm(ps_t[k][:, 0:256], pwb[:, k, :], og[:].rearrange("c b n -> c (b n)")).then_inc(s_off, 1)
            queries(1)
            pe.wait_ge(s_bd1, 2)
            pe.wait_ge(s_abd, 4)
            pe.wait_ge(s_fb3, 1)
            for i in range(2):
                mm(ps_mix[1][:, P * i:P * i + P], cas, bd1[:, i].rearrange("p a n -> p (a n)"), start=(i == 0))
            at_, bt_ = (abd[:, i].rearrange("p a n -> p (a n)") for i in (2, 3))
            mm(ps_mix[1][:, 2 * P:3 * P], at_, m1[:], start=False)
            mm(ps_mix[1][:, 3 * P:4 * P], bt_, m1[:], start=False, stop=False)
            mm(ps_mix[1][:, 3 * P:4 * P], at_, ident, start=False).then_inc(s_flps, 1)
            warm(ps_s[0], 1)
            for i in range(2):
                pe.wait_ge(s_wt, i + 1)
                for b in range(B):
                    for c in range(2):
                        last = pe.matmul(ps_mix[0][KEYS * c:KEYS * c + KEYS, KEYS * b:KEYS * b + KEYS],
                                         wt[:, i, b, :], xt[:, 2 * b + i, c:C:2], start=(b == 0 and i == 0),
                                         stop=(i == 1), skip_group_check=True, tile_position=(0, KEYS * c))
            last.then_inc(s_itps, 1)
            pe.wait_ge(s_qh2, 2)
            mm(ps_out[:, 0:P], late_ap("moT"), wmlp)
            mm(ps_out[:, P:2 * P], vec("ln_b").broadcast_to([C, P]), late_ap("mlp"), start=False).then_inc(s_gps, 1)
            pe.wait_ge(s_it, 1)
            pe.wait_ge(s_qh, 2)
            for bank_ in (ps_av, ps_t[1]):
                mm(bank_[:, 0:256], wvk, it[:, :, 0, :]).then_inc(s_kps, 1)
            pe.wait_ge(s_it, 2)
            pe.wait_ge(s_fl, 1)
            for b in range(B):
                last = mm(ps_mix[1][:, P * b:P * b + P], it[:, b].rearrange("c i n -> c (i n)"), wvv,
                          start=(b == 0))
            last.then_inc(s_vps, 1)
            warm(ps_s[0], 1)

            def scores_q(b):
                pe.wait_ge(*((s_kbr, b) if b else (s_kbr0, 1)))
                if b == 2:
                    pe.wait_ge(s_qh2, 2)
                if b >= 1:
                    pe.wait_ge(s_mx, 2 * b)
                for q in range(2):
                    mm(ps_s[q][:], qhr[:, b, q, :], kbr[:, b].rearrange("c i n -> c (i n)")).then_inc(s_s, 1)

            def scores_k(b, a):
                def product(i, k, q, start=False):
                    h = 4 * a + 2 * i
                    mm(ps_t[a][:, 256 * i:256 * i + 256], k[:, b, h:h + 2].rearrange("c i n -> c (i n)"),
                       q[:, b].rearrange("c a n -> c (a n)"), start=start, stop=False)

                if b == 0:
                    pe.wait_ge(s_kbd0, 1)
                    if a == 1:
                        pe.wait_ge(s_ksb, 1)
                    for i in range(2):
                        product(i, kbd, qh, start=(i == 0))
                    return
                pe.wait_ge(s_qlo, b // 2 + 1)
                pe.wait_ge(s_exp, 2 * b - 1 + a)
                for i in range(2):
                    product(i, kbr, qhr, start=(i == 0))
                    product(i, kbr, qlo)
                pe.wait_ge(s_klo, b)
                for i in range(2):
                    product(i, klo, qhr)

            def turn_max(b):
                pe.wait_ge(s_mx, 2 * b + 2)
                if b == 0:
                    pe.wait_ge(s_kbd0, 1)
                elif b == 1:
                    pe.wait_ge(s_vbd, 1)
                else:
                    pe.wait_ge(s_mxt, b)
                for q in range(2):
                    last = pe.transpose(turn_bank[b][0:HEADS, P * q:P * q + P], mx[:, b % 2, q], ident)
                last.then_inc(s_mxtps, 1)

            def shift(b):
                if b == 0:
                    pe.wait_ge(s_negpick, 1)
                pe.wait_ge(s_mxt, b + 1)
                for a in range(2):
                    for i in range(2):
                        n = P * (2 * a + i)
                        last = mm(ps_t[a][:, 256 * i:256 * i + 256], negpick[:, n:n + P], mxt[:, b % 2], start=False)
                    last.then_inc(s_st, 1)

            def values(b):
                if b == 0:
                    pe.wait_ge(s_vbd, 1)
                    pe.wait_ge(s_mxt, 1)
                elif b >= 2:
                    pe.wait_ge(s_at, b - 1)
                pe.wait_ge(s_exp, 2 * b + 2)
                for o, rhs in ((0, None), (256, const_ap("rowsum"))):
                    for i in range(4):
                        lhsT = rhs if rhs is not None else vbd[:, b, 32 * i:32 * i + 32]
                        last = pe.matmul(av_bank[b % 2][32 * i:32 * i + 32, o:o + 256], lhsT, pt[:, b % 2, i, :],
                                         start=(o == 0), stop=True, skip_group_check=True,
                                         tile_position=(0, 32 * i))
                last.then_inc(s_av, 1)

            def residual(b):
                pe.wait_ge(s_xcl, b // 2 + 1)
                if b == 0:
                    pe.wait_ge(s_g, 1)
                    pe.wait_ge(s_rows, 1)
                    pe.wait_ge(s_iwl, 1)
                elif b == 1:
                    pe.wait_ge(s_mxt, 4)
                else:
                    pe.wait_ge(s_mx, 8)
                for par in range(2):
                    t, o = 2 * b + par, out_bank[b][:, 256 * par:256 * par + 256]
                    mm(o, xch[:, t, :], iw[:, 0:2 * C], start=(par == 0), stop=False)
                    mm(o[:, C:2 * C], xch[:, t, :], iw[:, 2 * C:3 * C], start=False, stop=False)
                    mm(o, xcl[:, t, :], iw[:, 0:2 * C], start=False, stop=False)

            def project(b):
                pe.wait_ge(s_at, b + 1)
                for par in range(2):
                    last = mm(out_bank[b][:, 256 * par:256 * par + 256], at[:, b % 2, par], mo_g, start=False)
                last.then_inc(s_out, 1)

            def sums(g, par):
                if g == 0:
                    pe.wait_ge(s_exp, 8)
                else:
                    pe.wait_ge(s_at, 3 + par)
                for b in range(2):
                    pe.wait_ge(s_x1, 2 * g + b + 1)
                    n = 2 * (PAIRS[par] + FIXED[par])
                    last = mm(mix_bank[g][par][:, n * b:n * b + n], x1[:, 4 * g + 2 * b + par, :], wsd[:, par, 0:n],
                              start=(b == 0))
                last.then_inc(s_ctps[par], 1)

            def layer1(g, par):
                pe.wait_ge(s_ct[par], g + 1)
                n = PAIRS[par] + FIXED[par]
                t, r = halves(g, par)
                mm(t, w0, ct[:, g, par, :, 0:n])
                mm(r, w1, ct[:, g, par, :, n:2 * n], start=False).then_inc(s_tps[par], 1)

            def layer2(g, par):
                na, nf = PAIRS[par], FIXED[par]
                o = mix_bank[g][par][:, 0:256].rearrange("p (b n) -> p b n", b=2)
                pe.wait_ge(s_o1[par], 2 * g + 2)
                mm(o, wk, o1k[:, g, par], start=True, stop=False)
                src = o1n[:, g, par]
                if nf:
                    mm(o[:, :, na:na + nf], wn, src[:, :, na:na + nf], start=False)
                mm(o[:, :, 0:na], wn, src[:, :, na + nf:P], start=False)
                mm(o[:, :, na + nf:P], wn, src[:, :, 0:na], start=False).then_inc(s_yps[par], 1)

            def back_c(g, par):
                pe.wait_ge(s_ys[par], g + 1)
                for b in range(2):
                    last = mm(mix_bank[g][par][:, 256 + P * b:256 + P * b + P], ys[:, g, par, b, :], cas,
                              start=(b == 0))
                last.then_inc(s_ydps[par], 1)

            def back_w(g, par):
                pe.wait_ge(s_yd[par], g + 1)
                mm(mix_bank[g][par][:, 0:256], winv[:, par, :], yd[:, g, par].rearrange("p b n -> p (b n)")
                   ).then_inc(s_fps[par], 1)

            scores_q(0)
            scores_k(0, 0)
            residual(0)
            turn_max(0)
            scores_k(0, 1)
            for b in range(3):
                shift(b)
                if b == 0:
                    scores_q(1)
                if b >= 1:
                    values(b - 1)
                if b == 2:
                    project(0)
                scores_k(b + 1, 0)
                turn_max(b + 1)
                if b < 2:
                    scores_q(b + 2)
                scores_k(b + 1, 1)
            values(2)
            shift(3)
            residual(1)
            project(1)
            values(3)
            residual(2)
            project(2)
            residual(3)
            project(3)
            sums(0, 0)
            sums(0, 1)
            layer1(0, 0)
            layer1(0, 1)
            sums(1, 0)
            sums(1, 1)
            layer1(1, 0)
            layer1(1, 1)
            layer2(0, 0)
            layer2(0, 1)
            layer2(1, 0)
            back_c(0, 0)
            back_c(0, 1)
            layer2(1, 1)
            back_w(0, 0)
            back_w(0, 1)
            back_c(1, 0)
            back_c(1, 1)
            back_w(1, 0)
            back_w(1, 1)


def lay_out(x, i):
    f = np.ascontiguousarray
    x = np.asarray(x)
    x_tok = f(x.reshape(TILES, P, C).transpose(1, 0, 2))
    xr = x.reshape(B, 8, 2, 8, 2, C)
    x_chan = f(xr.transpose(5, 0, 2, 4, 1, 3).reshape(C, TILES, P))
    vecs = {"ln_g": i["L0_conv_ln_g"], "ln_b": i["L0_conv_ln_b"], "dw_b": i["L0_conv_dw_b"],
            "bq": i["L0_conv_bq"], "bv": i["L0_conv_bv"], "mq_b": i["L0_conv_mq_b"],
            "mk_b": i["L0_conv_mk_b"], "mv_b": i["L0_conv_mv_b"], "mo_b": i["L0_conv_mo_b"],
            "mlp_b": i["L0_conv_mlp_b"],
            "b1k": i["L1_conv_b1"][0], "b1n": i["L1_conv_b1"][1], "b2k": i["L1_conv_b2"][0],
            "b2n": i["L1_conv_b2"][1], "pw0": i["L0_conv_pw_w"][0], "pw1": i["L0_conv_pw_w"][1]}
    vecs = {n: np.asarray(v).reshape(C) for n, v in vecs.items()}
    image = lambda a: a.reshape(*a.shape[:-1], 8, 8, 2).swapaxes(-1, -2).reshape(a.shape)
    vecs["bq_img"] = image(vecs["bq"])
    early = np.concatenate([image(i["L0_conv_wq"]), i["L0_conv_dw_w"].reshape(C, NTAP),
                            np.stack([vecs[n] for n in VECTORS], axis=1)], axis=1)
    w1 = i["L1_conv_w1"].transpose(1, 2, 0, 3).reshape(C, 32)
    w2 = i["L1_conv_w2"].transpose(1, 2, 0, 3).reshape(C, 32)
    w2t = i["L1_conv_w2"].transpose(1, 3, 0, 2).reshape(C, 32)
    late = np.concatenate([i["L0_conv_wq"].T, i["L0_conv_mq_w"], i["L0_conv_wv"].T, i["L0_conv_mk_w"],
                           i["L0_conv_mv_w"], i["L0_conv_mo_w"].T, i["L0_conv_mlp_w"], w1, w2, w2t,
                           i["L0_conv_mo_w"]], axis=1)
    rows = np.concatenate([vecs[n] for n in ROWS])[None]
    return {"x_tok": x_tok, "x_chan": x_chan, "early": f(early), "late": f(late),
            "rows": f(rows), "const": constants(), "pick": picks()}


def kernel(**inputs):
    import concourse.bacc as bacc
    from concourse.bass_utils import run_bass_kernel_spmd as run

    inputs = {n: np.asarray(v) for n, v in inputs.items()}
    arrays = lay_out(inputs["x"], inputs)
    nc = bacc.Bacc("TRN2", target_bir_lowering=False, num_devices=1)
    args = [nc.dram_tensor(f"in_{n}", a.shape, F32, kind="ExternalInput").ap() for n, a in arrays.items()]
    out = nc.dram_tensor("out_tiles", (P, TILES, C), F32, kind="ExternalOutput").ap()
    build(nc, *args, out)
    r = run(nc, [{f"in_{n}": a for n, a in arrays.items()}], core_ids=[0])
    o = np.asarray(r.results[0]["out_tiles"]).reshape(2, 8, 8, B, 2, C)
    return np.ascontiguousarray(o.transpose(3, 1, 4, 2, 0, 5).reshape(B, H, W, C))
```
